# Optimizing a Trainium2 kernel written in Bass

```python
import numpy as np
import jax
import jax.numpy as jnp

def _softmax(x, axis=-1):
    return jax.nn.softmax(x, axis=axis)

def _gelu(x):
    return jax.nn.gelu(x, approximate=True)

def _silu(x):
    return jax.nn.silu(x)

def _sigmoid(x):
    return jax.nn.sigmoid(x)

def _layernorm(x, axis=-1, eps=1e-05):
    m = jnp.mean(x, axis=axis, keepdims=True)
    v = jnp.var(x, axis=axis, keepdims=True)
    return (x - m) / jnp.sqrt(v + eps)

def _scatter_add(tgt, idx, src, axis=0):
    return tgt.at[idx].add(src)

def _segment_sum(src, seg, n):
    return jax.ops.segment_sum(src, seg, n)
kernel_name = 'mk_xattn_ffn_d1_seqx_r8_e67ccd'

def setup_inputs(seed: int=0):
    np.random.seed(seed)
    _w = jnp.asarray

    def _rec_inputs():
        import jax
        import jax.numpy as jnp
        _rk = jax.random.key(seed)
        x = 6.313e-05 + 0.9998 * jax.random.normal(jax.random.fold_in(_rk, 1), (4, 512, 128), jnp.float32)
        _lenS = 512 - jax.random.randint(jax.random.fold_in(_rk, 7), (4,), 0, max(1, 512 // 4) + 1, jnp.int32)
        _lenS2 = 77 - jax.random.randint(jax.random.fold_in(_rk, 8), (4,), 0, max(1, 77 // 4) + 1, jnp.int32)
        _ctx_1024P = jax.random.normal(jax.random.fold_in(_rk, 11), (4, 16, 128), jnp.float32)
        _ctx_1024c = jax.random.dirichlet(jax.random.fold_in(_rk, 511), 0.3 * jnp.ones((16,), jnp.float32), (4, 77))
        _ctx_1024t = jnp.einsum('bsk,bkd->bsd', _ctx_1024c, _ctx_1024P)
        _ctx_1024t = _ctx_1024t * jax.lax.rsqrt(jnp.mean(jnp.square(_ctx_1024t)) + 1e-12) * 0.953939
        ctx_1024 = -0.000214406 + 1.00034 * (_ctx_1024t + 0.3 * jax.random.normal(jax.random.fold_in(_rk, 611), (4, 77, 128), jnp.float32))
        return (x, ctx_1024)
    x, ctx_1024 = _rec_inputs()

    def _L0_xattn_setup():
        import jax, jax.numpy as jnp
        import numpy as np
        from jax import lax
        BIG = jnp.float32(1e+30)

        def _pairwise_euclidean(a, b):
            aa = jnp.sum(a * a, axis=-1)[:, None]
            bb = jnp.sum(b * b, axis=-1)[None, :]
            ab = a @ b.T
            return jnp.sqrt(jnp.maximum(aa + bb - 2.0 * ab, 0.0))

        def _dtw_cost(D):
            row0 = jnp.cumsum(D[0])

            def row_step(prev_row, d_row):
                first = d_row[0] + prev_row[0]

                def col_step(left, inp):
                    d_ij, up, diag = inp
                    r = d_ij + jnp.minimum(jnp.minimum(up, left), diag)
                    return (r, r)
                _, rest = lax.scan(col_step, first, (d_row[1:], prev_row[1:], prev_row[:-1]))
                row = jnp.concatenate([first[None], rest])
                return (row, row)
            _, rows = lax.scan(row_step, row0, D[1:])
            return jnp.concatenate([row0[None], rows], axis=0)

        def _backtrack(R, T1, T2):
            L = T1 + T2 - 1

            def step(carry, _):
                i, j, done = carry
                valid = jnp.logical_not(done)
                cd = jnp.where((i > 0) & (j > 0), R[jnp.maximum(i - 1, 0), jnp.maximum(j - 1, 0)], BIG)
                cu = jnp.where(i > 0, R[jnp.maximum(i - 1, 0), j], BIG)
                cl = jnp.where(j > 0, R[i, jnp.maximum(j - 1, 0)], BIG)
                choice = jnp.argmin(jnp.stack([cd, cu, cl]))
                ni = jnp.where(choice <= 1, i - 1, i)
                nj = jnp.where((choice == 0) | (choice == 2), j - 1, j)
                at_origin = (i == 0) & (j == 0)
                ni = jnp.where(at_origin, 0, ni)
                nj = jnp.where(at_origin, 0, nj)
                return ((ni, nj, done | at_origin), (i, j, valid))
            init = (jnp.int32(T1 - 1), jnp.int32(T2 - 1), jnp.bool_(False))
            _, (i_idx, j_idx, valid) = lax.scan(step, init, None, length=L)
            return (i_idx, j_idx, valid)

        def _align_one(small, large):
            T_small, d = small.shape
            T_large = large.shape[0]
            D = _pairwise_euclidean(small, large)
            R = _dtw_cost(D)
            i_idx, j_idx, valid = _backtrack(R, T_small, T_large)
            contrib = small[i_idx] * valid[:, None].astype(small.dtype)
            expanded = jnp.zeros((T_large, d), dtype=small.dtype).at[j_idx].add(contrib)
            return expanded
        key = jax.random.key(seed)
        k1, k2 = jax.random.split(key)
        teacher = jax.random.normal(k1, (16, 50, 128), dtype=jnp.float32)
        student = jax.random.normal(k2, (16, 75, 128), dtype=jnp.float32)
        return {'teacher_features': teacher, 'student_features': student}
    _L0_xattn_all = _L0_xattn_setup()
    _L0_xattn_in = {k: v for k, v in _L0_xattn_all.items() if k in ()}
    del _L0_xattn_all

    def _L0_ffn_setup():
        import jax, jax.numpy as jnp
        import numpy as np
        H = 128
        I = 4 * H
        E = 8
        K = 2
        B, S = (2, 128)
        STD = 0.02 / np.sqrt(H)
        key = jax.random.key(seed)
        ks = jax.random.split(key, 8)
        x = jax.random.normal(ks[0], (B, S, H), dtype=jnp.float32)
        gate_w = jax.random.normal(ks[1], (H, E), dtype=jnp.float32) * STD
        bias = jnp.zeros((E,), dtype=jnp.float32)
        up_w = jax.random.normal(ks[2], (E, H, I), dtype=jnp.float32) * STD
        up_b = jnp.zeros((E, I), dtype=jnp.float32)
        down_w = jax.random.normal(ks[3], (E, I, H), dtype=jnp.float32) * STD
        down_b = jnp.zeros((E, H), dtype=jnp.float32)
        sw_up = jax.random.normal(ks[4], (H, I), dtype=jnp.float32) * STD
        sb_up = jnp.zeros((I,), dtype=jnp.float32)
        sw_down = jax.random.normal(ks[5], (I, H), dtype=jnp.float32) * STD
        sb_down = jnp.zeros((H,), dtype=jnp.float32)
        return {'x': x, 'gate_w': gate_w, 'bias': bias, 'up_w': up_w, 'up_b': up_b, 'down_w': down_w, 'down_b': down_b, 'sw_up': sw_up, 'sb_up': sb_up, 'sw_down': sw_down, 'sb_down': sb_down}
    _L0_ffn_all = _L0_ffn_setup()
    _L0_ffn_in = {k: v for k, v in _L0_ffn_all.items() if k in ('gate_w', 'bias', 'up_w', 'up_b', 'down_w', 'down_b', 'sw_up', 'sb_up', 'sw_down', 'sb_down')}
    del _L0_ffn_all
    return {'x': x, 'ctx_1024': ctx_1024, 'L0_ffn_gate_w': _L0_ffn_in['gate_w'], 'L0_ffn_bias': _L0_ffn_in['bias'], 'L0_ffn_up_w': _L0_ffn_in['up_w'], 'L0_ffn_up_b': _L0_ffn_in['up_b'], 'L0_ffn_down_w': _L0_ffn_in['down_w'], 'L0_ffn_down_b': _L0_ffn_in['down_b'], 'L0_ffn_sw_up': _L0_ffn_in['sw_up'], 'L0_ffn_sb_up': _L0_ffn_in['sb_up'], 'L0_ffn_sw_down': _L0_ffn_in['sw_down'], 'L0_ffn_sb_down': _L0_ffn_in['sb_down']}

def reference(x, ctx_1024, L0_ffn_gate_w, L0_ffn_bias, L0_ffn_up_w, L0_ffn_up_b, L0_ffn_down_w, L0_ffn_down_b, L0_ffn_sw_up, L0_ffn_sb_up, L0_ffn_sw_down, L0_ffn_sb_down):
    import jax
    import jax.numpy as jnp

    def _L0_xattn_ref(teacher_features, student_features):
        import jax, jax.numpy as jnp
        import numpy as np
        from jax import lax
        BIG = jnp.float32(1e+30)

        def _pairwise_euclidean(a, b):
            aa = jnp.sum(a * a, axis=-1)[:, None]
            bb = jnp.sum(b * b, axis=-1)[None, :]
            ab = a @ b.T
            return jnp.sqrt(jnp.maximum(aa + bb - 2.0 * ab, 0.0))

        def _dtw_cost(D):
            row0 = jnp.cumsum(D[0])

            def row_step(prev_row, d_row):
                first = d_row[0] + prev_row[0]

                def col_step(left, inp):
                    d_ij, up, diag = inp
                    r = d_ij + jnp.minimum(jnp.minimum(up, left), diag)
                    return (r, r)
                _, rest = lax.scan(col_step, first, (d_row[1:], prev_row[1:], prev_row[:-1]))
                row = jnp.concatenate([first[None], rest])
                return (row, row)
            _, rows = lax.scan(row_step, row0, D[1:])
            return jnp.concatenate([row0[None], rows], axis=0)

        def _backtrack(R, T1, T2):
            L = T1 + T2 - 1

            def step(carry, _):
                i, j, done = carry
                valid = jnp.logical_not(done)
                cd = jnp.where((i > 0) & (j > 0), R[jnp.maximum(i - 1, 0), jnp.maximum(j - 1, 0)], BIG)
                cu = jnp.where(i > 0, R[jnp.maximum(i - 1, 0), j], BIG)
                cl = jnp.where(j > 0, R[i, jnp.maximum(j - 1, 0)], BIG)
                choice = jnp.argmin(jnp.stack([cd, cu, cl]))
                ni = jnp.where(choice <= 1, i - 1, i)
                nj = jnp.where((choice == 0) | (choice == 2), j - 1, j)
                at_origin = (i == 0) & (j == 0)
                ni = jnp.where(at_origin, 0, ni)
                nj = jnp.where(at_origin, 0, nj)
                return ((ni, nj, done | at_origin), (i, j, valid))
            init = (jnp.int32(T1 - 1), jnp.int32(T2 - 1), jnp.bool_(False))
            _, (i_idx, j_idx, valid) = lax.scan(step, init, None, length=L)
            return (i_idx, j_idx, valid)

        def _align_one(small, large):
            T_small, d = small.shape
            T_large = large.shape[0]
            D = _pairwise_euclidean(small, large)
            R = _dtw_cost(D)
            i_idx, j_idx, valid = _backtrack(R, T_small, T_large)
            contrib = small[i_idx] * valid[:, None].astype(small.dtype)
            expanded = jnp.zeros((T_large, d), dtype=small.dtype).at[j_idx].add(contrib)
            return expanded
        return jax.vmap(_align_one)(teacher_features, student_features)

    def _L0_ffn_ref(x, gate_w, bias, up_w, up_b, down_w, down_b, sw_up, sb_up, sw_down, sb_down):
        import jax, jax.numpy as jnp
        import numpy as np
        H = 128
        I = 4 * H
        E = 8
        K = 2
        B, S = (2, 128)
        STD = 0.02 / np.sqrt(H)
        b, s, h = x.shape
        xf = x.reshape(-1, h)
        T = xf.shape[0]
        scores = jax.nn.sigmoid(xf @ gate_w + bias)
        top_scores, top_idx = jax.lax.top_k(scores, K)
        top_scores = top_scores / (jnp.sum(top_scores, axis=-1, keepdims=True) + 1e-06)
        w = jnp.zeros((T, E), dtype=xf.dtype).at[jnp.arange(T)[:, None], top_idx].add(top_scores)
        up = jnp.einsum('th,ehi->tei', xf, up_w) + up_b
        hact = jax.nn.gelu(up, approximate=False)
        eo = jnp.einsum('tei,eih->teh', hact, down_w) + down_b
        combined = jnp.einsum('teh,te->th', eo * 0.1, w)
        shared = (jax.nn.gelu(xf @ sw_up + sb_up, approximate=False) @ sw_down + sb_down) * 0.1
        out = (shared + combined).reshape(b, s, h)
        out = out / (jnp.max(jnp.abs(out), axis=-1, keepdims=True) + 1e-06)
        return out
    x = x + _L0_xattn_ref(ctx_1024, _layernorm(x, axis=-1))
    x = x + _L0_ffn_ref(_layernorm(x, axis=-1), L0_ffn_gate_w, L0_ffn_bias, L0_ffn_up_w, L0_ffn_up_b, L0_ffn_down_w, L0_ffn_down_b, L0_ffn_sw_up, L0_ffn_sb_up, L0_ffn_sw_down, L0_ffn_sb_down)
    return x

_drawn_inputs = setup_inputs


def setup_inputs(seed=0):
    import zlib

    import numpy as np

    out = dict(_drawn_inputs(seed))
    spreads = {'L0_ffn_bias': (0.0, 0.1),
     'L0_ffn_up_b': (0.0, 0.8),
     'L0_ffn_down_b': (0.0, 0.1),
     'L0_ffn_sb_up': (0.0, 0.8),
     'L0_ffn_sb_down': (0.0, 0.1)}
    factors = {'L0_ffn_up_w': 8.0, 'L0_ffn_down_w': 8.0, 'L0_ffn_sw_up': 8.0, 'L0_ffn_sw_down': 8.0}
    for name, (base, spread) in spreads.items():
        noise = np.random.default_rng([zlib.crc32(name.encode()), seed]).standard_normal(out[name].shape)
        drawn = base * np.exp(spread * noise) if base else spread * noise
        out[name] = jnp.asarray(drawn.astype(out[name].dtype))
    for name, factor in factors.items():
        out[name] = (out[name] * factor).astype(out[name].dtype)
    return out
```

```python
from contextlib import ExitStack

import concourse.bass as bass
from concourse import mybir

F32 = mybir.dt.float32
F16 = mybir.dt.float16
U32 = mybir.dt.uint32
ALU = mybir.AluOpType
ACT = mybir.ActivationFunctionType
AX_X = mybir.AxisListType.X

P = 128
B, S, H = 4, 512, 128
SMALL = 77
TILES = B * S // P
TPB = S // P
BLOCKS = 16
W = S // BLOCKS
STEPS = SMALL + BLOCKS - 1
LANES = B * BLOCKS
CHUNKS = 4
CHUNK = STEPS // CHUNKS
PAD = BLOCKS - 1
ROWS = SMALL + 2 * PAD
BIG = 1e30
EPS = 1e-5
E, TOP = 8, 2
I = 4 * H
NCH = I // P
SLOTS = 3
EXPERT_TILES = -(-((TOP * B * S + E * (P - 1)) // P) // SLOTS) * SLOTS
ROUNDS = EXPERT_TILES // SLOTS
WSCALE = 256.0
OUT_SCALE = 0.1


def build(nc, x, ctx_in, gate_w, gate_b, up_w, up_b, down_w, down_b, sw_up, sb_up, sw_down, sb_down, out):
    with ExitStack() as stack:
        def sb(name, shape, dt=F32):
            return stack.enter_context(nc.sbuf_tensor(name, shape, dt))

        def sem(name):
            return stack.enter_context(nc.semaphore(name))

        banks = [stack.enter_context(nc.psum_tensor(f"bank{i}", [P, 512], F32)) for i in range(8)]

        arena_a = sb("arena_a", [P, STEPS * (W + 1)])
        arena_b = sb("arena_b", [P, (STEPS + 1) * (W + 1)])
        arena_c = sb("arena_c", [P, STEPS * (W + 1)])
        arena_d = sb("arena_d", [P, STEPS * (W + 2)])
        dsk = arena_a[0:LANES, :].rearrange("l (s w) -> l s w", w=W + 1)
        cost = arena_b[0:LANES, :].rearrange("l (s w) -> l s w", w=W + 1)
        best = arena_c[0:LANES, :].rearrange("l (s w) -> l s w", w=W + 1)
        left = arena_d[0:LANES, :].rearrange("l (s w) -> l s w", w=W + 2)
        arena_e = sb("arena_e", [P, STEPS * W])
        arena_f = sb("arena_f", [P, STEPS * (W + 1)])
        arena_g = sb("arena_g", [P, (STEPS + 1) * (W + 1)])
        up = arena_e[0:LANES, :].rearrange("l (s w) -> l s w", w=W)
        leave = arena_f[0:LANES, :].rearrange("l (s w) -> l s w", w=W + 1)
        path = arena_g[0:LANES, :].rearrange("l (s w) -> l s w", w=W + 1)
        sent = sb("sent", [LANES, W + 1])
        inflow = sb("inflow", [LANES, W + 1])
        edge = sb("edge", [LANES, 2])
        ends = sb("ends", [LANES, 2, B])
        end_lane = sb("end_lane", [LANES, 2])
        big = sb("big", [PAD, S])

        x_sb = sb("x_sb", [P, TILES, H])
        ctx_sb = sb("ctx_sb", [SMALL, B, H])
        ident = sb("ident", [P, P])
        ones = sb("ones", [P, SMALL])
        eps = sb("eps", [P, 1])
        stats = sb("stats", [P, TILES, 6])
        mv = sb("mv", [P, TILES, 2])
        sd = sb("sd", [P, TILES])
        rstd = sb("rstd", [P, TILES])
        y = sb("y", [P, TILES, H])
        yT = sb("yT", [P, B, S])
        ysqT = sb("ysqT", [P, B, S])
        ctxm2T = sb("ctxm2T", [P, B, SMALL])
        ctxsq = sb("ctxsq", [SMALL, H])
        aa = sb("aa", [SMALL, B])
        dist = sb("dist", [SMALL, B, S])
        path_rows = dist
        x2 = sb("x2", [P, TILES, H])

        stage = sb("stage", [P, 2, I])
        up_hi = sb("up_hi", [P, (E + 1) * I], F16)
        up_lo = sb("up_lo", [P, (E + 1) * I], F16)
        down_hi = sb("down_hi", [P, (E + 1) * I], F16)
        down_lo = sb("down_lo", [P, (E + 1) * I], F16)
        gate_ld = sb("gate_ld", [P, E])
        gate_hi = sb("gate_hi", [P, E], F16)
        gate_lo = sb("gate_lo", [P, E], F16)
        gate_b_sb = sb("gate_b_sb", [P, E])
        bias_ld = sb("bias_ld", [64, I])
        bias_hi = sb("bias_hi", [64, I], F16)
        bias_rows = sb("bias_rows", [P, I], F16)
        expert_sel = sb("expert_sel", [P, E * P], F16)
        sb_upT = sb("sb_upT", [P, NCH])
        down_b_all = sb("down_b_all", [E + 1, H])

        rank_key = sb("rank_key", [P, E])
        logits = sb("logits", [P, TILES, E])
        score = sb("score", [P, TILES, E])
        score2 = sb("score2", [P, TILES, E])
        top = sb("top", [P, TOP, TILES])
        is_top = sb("is_top", [P, TILES, E])
        key = sb("key", [P, TILES, E])
        key_top = sb("key_top", [P, TILES])
        pick = sb("pick", [P, TOP, TILES, E])
        picked = sb("picked", [P, TILES, E], F16)
        denom = sb("denom", [P, TILES])
        weight = sb("weight", [P, TOP, TILES])
        part = sb("part", [P, TOP, TILES, E])
        gates = sb("gates", [P, TILES, E + 1])
        before = sb("before", [P, P], F16)
        ones16 = sb("ones16", [P, P], F16)
        carry_on = sb("carry_on", [P, E, TILES])
        thresholds = sb("thresholds", [P, TILES])
        tile_no = sb("tile_no", [1, EXPERT_TILES])
        in_tile = sb("in_tile", [P, E, TILES])
        running = sb("running", [P, E, TILES])
        offset = sb("offset", [P, E, TILES])
        exceeds = sb("exceeds", [P, E, TILES])
        tiles_of = sb("tiles_of", [P, E])
        tiles_upto = sb("tiles_upto", [P, E])
        tiles_before = sb("tiles_before", [P, E])
        place = sb("place", [P, TILES, E])
        slot_f = sb("slot_f", [P, TOP, TILES])
        slot = sb("slot", [P, TOP * TILES], U32)
        past = sb("past", [1, EXPERT_TILES, E])
        tile_expert_f = sb("tile_expert_f", [1, EXPERT_TILES])
        tile_expert = sb("tile_expert", [1, EXPERT_TILES], U32)

        yT_hi = arena_a[:, 0:TILES * P // 2].bitcast(F16)
        yT_lo = arena_a[:, TILES * P // 2:TILES * P].bitcast(F16)
        gathered = arena_b[:, 0:TILES * H], arena_c[:, 0:TILES * H]
        acc = arena_d[:, 0:TILES * H]
        gatesT = ysqT[0:E + 1, :, :].rearrange("e b s -> e (b s)")

        def within(arena, start, shape, dt=F32):
            n = 1
            for m in shape:
                n *= m
            n = n // 2 if dt == F16 else n
            view = arena[:, start:start + n]
            view = view.bitcast(F16) if dt == F16 else view
            names = " ".join("abc"[:len(shape)])
            sizes = dict(zip("abc", shape))
            return view.rearrange(f"p ({names}) -> p {names}", **sizes), start + n

        x_flat = x_sb[:].rearrange("p n d -> p (n d)")
        yT_flat = yT[:].rearrange("p b s -> p (b s)")
        total, at = within(x_flat, 0, (2, TPB, H))
        result, at = within(x_flat, at, (2, TPB, H))
        hid, at = within(yT_flat, 0, (SLOTS, I))
        x_row, at = within(yT_flat, at, (SLOTS, H))
        shared_hi, at = within(arena_e, 0, (2, NCH, S), F16)
        y_row, at = within(arena_e, at, (SLOTS, H))
        xT_hi, at = within(arena_e, at, (SLOTS, P), F16)
        xT_lo, at = within(arena_e, at, (SLOTS, P), F16)
        shared_lo, at = within(arena_f, 0, (2, NCH, S), F16)
        hid_hi, at = within(arena_f, at, (SLOTS, I), F16)
        hid_lo, at = within(arena_g, 0, (SLOTS, I), F16)
        shared_g, at = within(arena_g, at, (2, S))
        zeros = sb("zeros", [P, H])
        peak = sb("peak", [P, B, TPB])
        peak_eps = sb("peak_eps", [P, B, TPB])
        inv_peak = sb("inv_peak", [P, B, TPB])

        dist_dram = nc.dram_tensor("dist_dram", (B, ROWS, S), F32, kind="Internal")
        path_dram = nc.dram_tensor("path_dram", (B, ROWS, S), F32, kind="Internal")
        sorted_dram = nc.dram_tensor("sorted_dram", (EXPERT_TILES * P, H), F32, kind="Internal")
        expert_dram = nc.dram_tensor("expert_dram", (EXPERT_TILES * P, H), F32, kind="Internal")

        x_in = [sem(f"x_in{b}") for b in range(B)]
        ctx_ld = sem("ctx_ld")
        small_ld = sem("small_ld")
        stage_ld = [sem(f"stage_ld{i}") for i in range(2)]
        const_ready = sem("const_ready")
        pads_ready = sem("pads_ready")
        big_ready = sem("big_ready")
        ffn_const_ready = sem("ffn_const_ready")
        pool_step = sem("pool_step")
        stats_ready = sem("stats_ready")
        var_ready = sem("var_ready")
        sd_ready = sem("sd_ready")
        rstd_ready = sem("rstd_ready")
        y_ready = sem("y_ready")
        yT_in_psum = sem("yT_in_psum")
        yT_ready = sem("yT_ready")
        ctxT_in_psum = sem("ctxT_in_psum")
        ctxT_ready = sem("ctxT_ready")
        aa_ready = sem("aa_ready")
        d2_in_psum = sem("d2_in_psum")
        d2_ready = sem("d2_ready")
        dist_ready = sem("dist_ready")
        pad_out = sem("pad_out")
        dist_out = sem("dist_out")
        dsk_in = [sem(f"dsk_in{k}") for k in range(CHUNKS)]
        lanes_ready = sem("lanes_ready")
        edge_ready = sem("edge_ready")
        best_ready = sem("best_ready")
        cost_ready = sem("cost_ready")
        mask_ready = sem("mask_ready")
        inflow_ready = sem("inflow_ready")
        sent_ready = sem("sent_ready")
        path_ready = sem("path_ready")
        path_out = sem("path_out")
        rows_in = [sem(f"rows_in{b}") for b in range(B)]
        added_in_psum = sem("added_in_psum")
        x2_ready = sem("x2_ready")
        scaled_ready = sem("scaled_ready")
        halves_hi = sem("halves_hi")
        halves_lo = sem("halves_lo")
        small_hi = sem("small_hi")
        weights_ready = sem("weights_ready")
        stats2_ready = sem("stats2_ready")
        var2_ready = sem("var2_ready")
        sd2_ready = sem("sd2_ready")
        rstd2_ready = sem("rstd2_ready")
        y2_ready = sem("y2_ready")
        y2T_in_psum = sem("y2T_in_psum")
        y2T_hi_ready = sem("y2T_hi_ready")
        y2T_lo_ready = sem("y2T_lo_ready")
        logits_in_psum = sem("logits_in_psum")
        logits_ready = sem("logits_ready")
        score_ready = sem("score_ready")
        route = sem("route")
        picked_ready = sem("picked_ready")
        ranks_in_psum = sem("ranks_in_psum")
        gates_ready = sem("gates_ready")
        gatesT_in_psum = sem("gatesT_in_psum")
        gatesT_ready = sem("gatesT_ready")
        slots_ready = sem("slots_ready")
        table_ready = sem("table_ready")
        zeroed = sem("zeroed")
        scattered = sem("scattered")
        x_row_in = [sem(f"x_row_in{k}") for k in range(SLOTS)]
        xT_in_psum = sem("xT_in_psum")
        xT_hi_ready = sem("xT_hi_ready")
        xT_ready = sem("xT_ready")
        up_done = sem("up_done")
        gelu_done = sem("gelu_done")
        hid_hi_ready = sem("hid_hi_ready")
        hid_ready = sem("hid_ready")
        y_done = sem("y_done")
        y_row_ready = sem("y_row_ready")
        y_row_out = [sem(f"y_row_out{k}") for k in range(SLOTS)]
        s_up_done = sem("s_up_done")
        s_gelu_done = sem("s_gelu_done")
        s_hi_ready = sem("s_hi_ready")
        s_hid_ready = sem("s_hid_ready")
        s_down_done = sem("s_down_done")
        acc_ready = sem("acc_ready")
        gather_in = [sem(f"gather_in{b}") for b in range(B)]
        total_step = sem("total_step")
        tail = sem("tail")
        result_ready = sem("result_ready")
        out_done = [sem(f"out_done{i}") for i in range(2)]

        x_tiles = x.rearrange("b (n p) d -> b p n d", p=P)
        out_tiles = out.rearrange("b (n p) d -> b p n d", p=P)
        UP_BANK, XT_BANK, Y_BANK, S_UP_BANK, S_DOWN_BANK = 0, 3, 4, 5, 7

        def batch_tiles(b):
            return slice(b * TPB, (b + 1) * TPB)

        def skewed(dram, b, s0, s1):
            last = BLOCKS - 1
            return bass.AP(tensor=dram, offset=(b * ROWS + PAD + s0 - last) * S + last * W,
                           ap=[[S - W, BLOCKS], [S, s1 - s0], [1, W]])

        block = stack.enter_context(nc.Block())

        @block.sync
        def _(sp):
            for b in range(B):
                sp.dma_start(x_sb[:, batch_tiles(b), :], x_tiles[b]).then_inc(x_in[b], 16)
            sp.wait_ge(big_ready, 1)
            for b in range(B):
                for edge_rows in (slice(0, PAD), slice(PAD + SMALL, ROWS)):
                    sp.dma_start(dist_dram.ap()[b, edge_rows, :], big[:]).then_inc(pad_out, 16)
            for b in range(B):
                sp.wait_ge(dist_ready, b + 1)
                sp.dma_start(dist_dram.ap()[b, PAD:PAD + SMALL, :], dist[:, b, :]).then_inc(dist_out, 16)
            sp.wait_ge(pad_out, 16 * 2 * B)
            sp.wait_ge(dist_out, 16 * B)
            for k in range(CHUNKS):
                for b in range(B):
                    steps = slice(k * CHUNK, (k + 1) * CHUNK)
                    sp.dma_start(dsk[b * BLOCKS:(b + 1) * BLOCKS, steps, 1:W + 1],
                                 skewed(dist_dram, b, steps.start, steps.stop)).then_inc(dsk_in[k], 16)
            for b in (bias_ld[0:E, :], bias_ld[32:32 + E, :]):
                sp.dma_start(b, up_b).then_inc(small_ld, 16)
            sp.dma_start(gate_ld[:], gate_w).then_inc(small_ld, 16)
            sp.dma_start(gate_b_sb[:], gate_b.partition_broadcast(P)).then_inc(small_ld, 16)
            sp.dma_start(down_b_all[0:E, :], down_b).then_inc(small_ld, 16)
            sp.dma_start(down_b_all[E:E + 1, :], sb_down.rearrange("(a d) -> a d", a=1)).then_inc(small_ld, 16)
            with nc.allow_non_contiguous_dma(reason="512 numbers, once"):
                sp.dma_start(sb_upT[:], sb_up.rearrange("(c p) -> p c", p=P)).then_inc(small_ld, 16)
            sp.wait_ge(ffn_const_ready, 1)
            sp.dma_start(sorted_dram.ap().rearrange("(j p) d -> p j d", p=P),
                         zeros[:].unsqueeze(1).to_broadcast([P, EXPERT_TILES, H])).then_inc(zeroed, 16)
            for e in range(E + 1):
                for m in range(2):
                    n = 2 * e + m
                    if n >= 2:
                        sp.wait_ge(halves_lo, n - 1)
                    if m == 0:
                        sp.dma_start(stage[:, 0, :], up_w[e] if e < E else sw_up).then_inc(stage_ld[0], 16)
                    else:
                        src = down_w[e] if e < E else sw_down
                        sp.dma_start(stage[:, 1, :].rearrange("p (c d) -> p c d", d=H),
                                     src.rearrange("(c p) d -> p c d", p=P)).then_inc(stage_ld[1], 16)
            for k in reversed(range(CHUNKS)):
                sp.wait_ge(path_ready, STEPS - k * CHUNK)
                for b in range(B):
                    steps = slice(k * CHUNK, (k + 1) * CHUNK)
                    sp.dma_start(skewed(path_dram, b, steps.start, steps.stop),
                                 path[b * BLOCKS:(b + 1) * BLOCKS, steps, 0:W]).then_inc(path_out, 16)
            sp.wait_ge(path_out, 16 * B * CHUNKS)
            for b in range(B):
                sp.dma_start(path_rows[:, b, :], path_dram.ap()[b, PAD:PAD + SMALL, :]).then_inc(rows_in[b], 16)

            def load(j, k):
                sp.dma_start(x_row[:, k, :], sorted_dram.ap()[bass.ds(j * P, P), :]).then_inc(x_row_in[k], 16)

            def store(j, k):
                sp.wait_ge(y_row_ready, j + 1)
                sp.dma_start(expert_dram.ap()[bass.ds(j * P, P), :], y_row[:, k, :]).then_inc(y_row_out[k], 16)

            sp.wait_ge(scattered, 16 * TOP * TILES)
            for k in range(SLOTS):
                load(k, k)
            for k in range(SLOTS):
                sp.wait_ge(xT_in_psum, k + 1)
                load(SLOTS + k, k)
                if k == 2:
                    store(0, 0)
            with sp.Fori(1, ROUNDS - 1) as i:
                for k in range(SLOTS):
                    sp.wait_ge(xT_in_psum, i * SLOTS + (k + 1))
                    load(i * SLOTS + (k + SLOTS), k)
                    store(i * SLOTS + (k - 2), (k - 2) % SLOTS)
            for j in range(EXPERT_TILES - SLOTS - 2, EXPERT_TILES):
                store(j, j % SLOTS)
            for b in range(B):
                sp.wait_ge(result_ready, b + 1)
                sp.dma_start(out_tiles[b], result[:, b % 2, :, :]).then_inc(out_done[b % 2], 16)
            for i in range(2):
                sp.wait_ge(out_done[i], 16 * B // 2)

        @block.gpsimd
        def _(pool):
            pool.memset(ident[:], 0.0).then_inc(pool_step, 1)
            pool.memset(ones[:], 1.0)
            pool.memset(eps[:], EPS)
            pool.wait_ge(pool_step, 1)
            pool.affine_select(out=ident[:], in_=ident[:], compare_op=ALU.not_equal, fill=1.0, base=0,
                               pattern=[[-1, P]], channel_multiplier=1).then_inc(const_ready, 1)
            pool.memset(big[:], BIG).then_inc(big_ready, 1)
            pool.memset(best[:, :, 0], BIG)
            pool.memset(cost[:, 0, :], BIG)
            pool.memset(ends[:], 0.0).then_inc(pool_step, 1)
            pool.wait_ge(pool_step, 2)
            for e in range(2):
                last = pool.affine_select(out=ends[:, e, :], in_=ends[:, e, :], compare_op=ALU.not_equal, fill=1.0,
                                          base=(e - 1) * (BLOCKS - 1), pattern=[[-BLOCKS, B]], channel_multiplier=1)
            last.then_inc(pads_ready, 1)
            for e in range(E):
                pool.memset(rank_key[:, e:e + 1], float(E - e))
            pool.memset(gates[:, :, E], WSCALE)
            pool.memset(zeros[:], 0.0)
            pool.memset(bias_rows[:], 0.0)
            pool.memset(expert_sel[:], 0.0)
            pool.memset(before[:], 1.0)
            pool.memset(ones16[:], 1.0)
            pool.memset(carry_on[:], 1.0)
            pool.iota(thresholds[:], pattern=[[P, TILES]], base=0, channel_multiplier=0,
                      allow_small_or_imprecise_dtypes=True)
            pool.iota(tile_no[:], pattern=[[1, EXPERT_TILES]], base=0, channel_multiplier=0,
                      allow_small_or_imprecise_dtypes=True).then_inc(pool_step, 1)
            pool.wait_ge(pool_step, 3)
            pool.memset(carry_on[:, :, 0], 0.0)
            pool.affine_select(out=before[:], in_=before[:], compare_op=ALU.is_ge, fill=0.0, base=-1,
                               pattern=[[1, P]], channel_multiplier=-1)
            sel = expert_sel[:].rearrange("p (e t) -> p e t", e=E)
            pool.affine_select(out=sel, in_=sel, compare_op=ALU.not_equal, fill=1.0, base=0,
                               pattern=[[-1, E], [0, P]], channel_multiplier=1).then_inc(pool_step, 1)
            pool.wait_ge(pool_step, 4)
            pool.affine_select(out=sel, in_=sel, compare_op=ALU.not_equal, fill=1.0, base=-32,
                               pattern=[[-1, E], [0, P]], channel_multiplier=1).then_inc(ffn_const_ready, 1)
            pool.wait_ge(small_hi, 1)
            pool.tensor_tensor(bias_rows[32:32 + E, :], bias_ld[32:32 + E, :], bias_hi[32:32 + E, :], ALU.subtract
                               ).then_inc(pool_step, 1)
            pool.wait_ge(pool_step, 5)
            pool.tensor_tensor(gate_lo[:], gate_ld[:], gate_hi[:], ALU.subtract).then_inc(weights_ready, 1)
            for e in range(E + 1):
                cols = slice(e * I, (e + 1) * I)
                for m, (hi, lo) in enumerate(((up_hi, up_lo), (down_hi, down_lo))):
                    pool.wait_ge(halves_hi, 2 * e + m + 1)
                    pool.tensor_tensor(lo[:, cols], stage[:, m, :], hi[:, cols], ALU.subtract).then_inc(halves_lo, 1)
            pool.wait_ge(zeroed, 16)
            pool.wait_ge(slots_ready, 1)
            for t in range(TILES):
                for k in range(TOP):
                    pool.indirect_dma_start(
                        out=sorted_dram.ap(), in_=y[:, t, :], in_offset=None,
                        out_offset=bass.IndirectOffsetOnAxis(ap=slot[:, k * TILES + t:k * TILES + t + 1], axis=0)
                    ).then_inc(scattered, 16)
            for k in range(SLOTS):
                pool.wait_ge(y_row_out[k], 16 * ROUNDS)
            for t in range(TILES):
                for k in range(TOP):
                    pool.indirect_dma_start(
                        out=gathered[k][:, t * H:(t + 1) * H], in_=expert_dram.ap(), out_offset=None,
                        in_offset=bass.IndirectOffsetOnAxis(ap=slot[:, k * TILES + t:k * TILES + t + 1], axis=0)
                    ).then_inc(gather_in[t // TPB], 16)

        @block.scalar
        def _(act):
            act.dma_start(ctx_sb[:], ctx_in.rearrange("b i d -> i b d")).then_inc(ctx_ld, 16)
            act.wait_ge(ctx_ld, 16)
            for b in range(B):
                act.activation(ctxsq[:], ctx_sb[:, b, :], ACT.Square, accum_out=aa[:, b:b + 1]).then_inc(aa_ready, 1)
                act.wait_ge(aa_ready, b + 1)
            act.wait_ge(ctxT_in_psum, 1)
            act.mul(ctxm2T[:].rearrange("p b i -> p (b i)"), banks[7][:, 0:B * SMALL], -2.0).then_inc(ctxT_ready, 1)
            act.wait_ge(const_ready, 1)
            for b in range(B):
                t = batch_tiles(b)
                act.wait_ge(var_ready, b + 1)
                act.activation(sd[:, t], mv[:, t, 1], ACT.Sqrt, bias=eps[:]).then_inc(sd_ready, 1)
            for b in range(B):
                act.wait_ge(yT_in_psum, b + 1)
                act.activation(yT[:, b, :], banks[b][:], ACT.Copy).then_inc(yT_ready, 1)
                act.activation(ysqT[:, b, :], banks[b][:], ACT.Square).then_inc(yT_ready, 1)
            for b in range(B):
                act.wait_ge(d2_ready, b + 1)
                act.activation(dist[:, b, :], dist[:, b, :], ACT.Sqrt).then_inc(dist_ready, 1)
            act.wait_ge(small_ld, 16 * 7)
            act.wait_ge(ffn_const_ready, 1)
            for rows in (slice(0, E), slice(32, 32 + E)):
                act.mul(bias_ld[rows, :], bias_ld[rows, :], WSCALE).then_inc(scaled_ready, 1)
            act.mul(gate_ld[:], gate_ld[:], WSCALE).then_inc(scaled_ready, 1)
            act.wait_ge(scaled_ready, 3)
            act.activation(bias_rows[0:E, :], bias_ld[0:E, :], ACT.Copy)
            act.activation(bias_hi[32:32 + E, :], bias_ld[32:32 + E, :], ACT.Copy)
            act.activation(gate_hi[:], gate_ld[:], ACT.Copy).then_inc(small_hi, 1)
            for e in range(E + 1):
                cols = slice(e * I, (e + 1) * I)
                for m, hi in enumerate((up_hi, down_hi)):
                    n = 2 * e + m
                    act.wait_ge(stage_ld[m], 16 * (e + 1))
                    act.mul(stage[:, m, :], stage[:, m, :], WSCALE).then_inc(scaled_ready, 1)
                    act.wait_ge(scaled_ready, n + 4)
                    act.activation(hi[:, cols], stage[:, m, :], ACT.Copy).then_inc(halves_hi, 1)
            for b in range(B):
                t = batch_tiles(b)
                act.wait_ge(var2_ready, b + 1)
                act.activation(sd[:, t], mv[:, t, 1], ACT.Sqrt, bias=eps[:]).then_inc(sd2_ready, 1)
            for b in range(B):
                act.wait_ge(y2T_in_psum, b + 1)
                act.activation(yT_hi[:, b * S:(b + 1) * S], banks[4 + b][:], ACT.Copy).then_inc(y2T_hi_ready, 1)
            act.wait_ge(logits_ready, 1)
            act.activation(score[:], logits[:], ACT.Sigmoid).then_inc(score_ready, 1)
            act.wait_ge(gatesT_in_psum, 1)
            for b in range(B):
                act.activation(gatesT[:, b * S:(b + 1) * S], banks[b][0:E + 1, :], ACT.Copy).then_inc(gatesT_ready, 1)

            def shared_pair(q):
                for n in range(2 * q * NCH, (2 * q + 2) * NCH):
                    act.wait_ge(s_up_done, n + 1)
                    if n >= 2:
                        act.wait_ge(s_hid_ready, n - 1)
                    act.activation(shared_g[:, n % 2, :], banks[S_UP_BANK + n % 2][:], ACT.Gelu,
                                   bias=sb_upT[:, n % NCH:n % NCH + 1], scale=1.0 / WSCALE).then_inc(s_gelu_done, 1)

            def x_high(j, k):
                act.wait_ge(xT_in_psum, j + 1)
                act.activation(xT_hi[:, k, :], banks[XT_BANK][:, 0:P], ACT.Copy).then_inc(xT_hi_ready, 1)

            def gelu(j, k, first=False):
                act.wait_ge(up_done, j + 1)
                if not first:
                    act.wait_ge(hid_ready, j - 2)
                act.activation(hid[:, k, :], banks[UP_BANK + k][:], ACT.Gelu, scale=1.0 / WSCALE
                               ).then_inc(gelu_done, 1)

            def y_copy(j, k, i, first=False):
                act.wait_ge(y_done, j + 1)
                if not first:
                    act.wait_ge(y_row_out[k], i * 16)
                act.activation(y_row[:, k, :], banks[Y_BANK][:, 0:H], ACT.Copy).then_inc(y_row_ready, 1)

            shared_pair(0)
            x_high(0, 0)
            x_high(1, 1)
            for k in range(SLOTS):
                gelu(k, k, first=True)
                x_high(k + 2, (k + 2) % SLOTS)
                if k == 2:
                    y_copy(0, 0, 0, first=True)
            for j in range(SLOTS, 2 * SLOTS):
                gelu(j, j % SLOTS)
                x_high(j + 2, (j + 2) % SLOTS)
                y_copy(j - 2, (j - 2) % SLOTS, 1, first=(j - 2 < SLOTS))
            with act.Fori(2, ROUNDS - 1) as i:
                for k in range(SLOTS):
                    j = i * SLOTS + k
                    gelu(j, k)
                    x_high(j + 2, (k + 2) % SLOTS)
                    y_copy(j - 2, (k - 2) % SLOTS, i - 1 if k < 2 else i)
            for j in range(EXPERT_TILES - SLOTS, EXPERT_TILES + 2):
                if j < EXPERT_TILES:
                    gelu(j, j % SLOTS)
                if j + 2 < EXPERT_TILES:
                    x_high(j + 2, (j + 2) % SLOTS)
                y_copy(j - 2, (j - 2) % SLOTS, (j - 2) // SLOTS)
            shared_pair(1)

        @block.tensor
        def _(pe):
            pe.wait_ge(const_ready, 1)
            pe.wait_ge(ctx_ld, 16)
            for b in range(B):
                mm = pe.transpose(banks[7][:, b * SMALL:(b + 1) * SMALL], ctx_sb[:, b, :], ident[0:SMALL, 0:SMALL])
            mm.then_inc(ctxT_in_psum, 1)
            for b in range(B):
                for n in range(TPB):
                    pe.wait_ge(y_ready, b * TPB + n + 1)
                    mm = pe.transpose(banks[b][:, n * P:(n + 1) * P], y[:, b * TPB + n, :], ident[:])
                mm.then_inc(yT_in_psum, 1)
            pe.wait_ge(ctxT_ready, 1)
            for b in range(B):
                pe.wait_ge(yT_ready, 2 * b + 2)
                pe.matmul(banks[4 + b][0:SMALL, :], ctxm2T[:, b, :], yT[:, b, :], start=True, stop=False)
                pe.matmul(banks[4 + b][0:SMALL, :], ones[:], ysqT[:, b, :], start=False, stop=True
                          ).then_inc(d2_in_psum, 1)
            for b in range(B):
                pe.wait_ge(rows_in[b], 16)
                for n in range(TPB):
                    mm = pe.matmul(banks[b][:, n * P:(n + 1) * P], path_rows[:, b, n * P:(n + 1) * P],
                                   ctx_sb[:, b, :], start=True, stop=True)
                mm.then_inc(added_in_psum, 1)
            for b in range(B):
                pe.wait_ge(y2_ready, b + 1)
                for n in range(TPB):
                    mm = pe.transpose(banks[4 + b][:, n * P:(n + 1) * P], y[:, b * TPB + n, :], ident[:])
                mm.then_inc(y2T_in_psum, 1)
            pe.wait_ge(weights_ready, 1)
            pe.wait_ge(x2_ready, B)
            for t in range(TILES):
                cols = slice(t * P, (t + 1) * P)
                if t % TPB == 0:
                    pe.wait_ge(y2T_lo_ready, t // TPB + 1)
                o = banks[0][:, t * E:(t + 1) * E]
                pe.matmul(o, yT_hi[:, cols], gate_hi[:], start=True, stop=False)
                pe.matmul(o, yT_hi[:, cols], gate_lo[:], start=False, stop=False)
                mm = pe.matmul(o, yT_lo[:, cols], gate_hi[:], start=False, stop=True)
            mm.then_inc(logits_in_psum, 1)
            pe.wait_ge(picked_ready, 1)
            chosen = picked[:].rearrange("p n e -> p (n e)")
            pe.matmul(banks[4][:, 0:P], before[:], chosen, start=True, stop=True)
            pe.matmul(banks[5][:, 0:P], ones16[:], chosen, start=True, stop=True).then_inc(ranks_in_psum, 1)
            pe.wait_ge(gates_ready, 1)
            for t in range(TILES):
                mm = pe.transpose(banks[t // TPB][0:E + 1, t % TPB * P:(t % TPB + 1) * P], gates[:, t, :], ident[:])
            mm.then_inc(gatesT_in_psum, 1)
            pe.wait_ge(halves_lo, 2 * (E + 1))
            pe.wait_ge(slots_ready, 1)

            def three_passes(o, a_hi, a_lo, b_hi, b_lo, start, stop):
                pe.matmul(o, a_hi, b_hi, start=start, stop=False)
                pe.matmul(o, a_hi, b_lo, start=False, stop=False)
                return pe.matmul(o, a_lo, b_hi, start=False, stop=stop)

            def shared_up(b):
                for c in range(NCH):
                    n = b * NCH + c
                    if n >= 2:
                        pe.wait_ge(s_gelu_done, n - 1)
                    w = slice(E * I + c * P, E * I + (c + 1) * P)
                    t = slice(b * S, (b + 1) * S)
                    three_passes(banks[S_UP_BANK + n % 2][:], up_hi[:, w], up_lo[:, w], yT_hi[:, t], yT_lo[:, t],
                                 True, True).then_inc(s_up_done, 1)

            def shared_down(b):
                pe.wait_ge(s_hid_ready, (b + 1) * NCH)
                pe.wait_ge(gatesT_ready, B)
                if b:
                    pe.wait_ge(acc_ready, b)
                for n in range(TPB):
                    o = banks[S_DOWN_BANK][:, n * H:(n + 1) * H]
                    t = b * TPB + n
                    pe.matmul(o, gatesT[:, t * P:(t + 1) * P], down_b_all[:], start=True, stop=False)
                    for c in range(NCH):
                        w = slice(E * I + c * P, E * I + (c + 1) * P)
                        h = slice(n * P, (n + 1) * P)
                        mm = three_passes(o, shared_hi[:, b % 2, c, h], shared_lo[:, b % 2, c, h],
                                          down_hi[:, w], down_lo[:, w], False, c == NCH - 1)
                mm.then_inc(s_down_done, 1)

            def shared_pair(q):
                for b in (2 * q, 2 * q + 1):
                    shared_up(b)
                for b in (2 * q, 2 * q + 1):
                    shared_down(b)

            def turn(j, k, r):
                pe.wait_ge(x_row_in[k], (r + 1) * 16)
                pe.transpose(banks[XT_BANK][:, 0:P], x_row[:, k, :], ident[:]).then_inc(xT_in_psum, 1)

            def expert(j):
                return pe.value_load(tile_expert[0:1, bass.ds(j, 1)], min_val=0, max_val=E - 1)

            def up(j, k, first=False):
                e = expert(j)
                pe.wait_ge(xT_ready, j + 1)
                if not first:
                    pe.wait_ge(gelu_done, j - 2)
                for c in range(NCH):
                    o = banks[UP_BANK + k][:, c * P:(c + 1) * P]
                    pe.matmul(o, bias_rows[:, c * P:(c + 1) * P], expert_sel[:, bass.ts(e, P)], start=True, stop=False)
                    w = bass.ds(e * I + c * P, P)
                    mm = three_passes(o, up_hi[:, w], up_lo[:, w], xT_hi[:, k, :], xT_lo[:, k, :], False, True)
                mm.then_inc(up_done, 1)

            def down(j, k, first=False):
                e = expert(j)
                pe.wait_ge(hid_ready, j + 1)
                if not first:
                    pe.wait_ge(y_row_ready, j)
                for c in range(NCH):
                    w = bass.ds(e * I + c * P, P)
                    h = slice(c * P, (c + 1) * P)
                    mm = three_passes(banks[Y_BANK][:, 0:H], hid_hi[:, k, h], hid_lo[:, k, h], down_hi[:, w],
                                      down_lo[:, w], c == 0, c == NCH - 1)
                mm.then_inc(y_done, 1)

            def later_turn(j, k, r):
                pe.wait_ge(xT_ready, j)
                turn(j, k, r)

            shared_pair(0)
            pe.wait_ge(table_ready, 1)
            turn(0, 0, 0)
            later_turn(1, 1, 0)
            for j in range(SLOTS):
                up(j, j, first=True)
                later_turn(j + 2, (j + 2) % SLOTS, (j + 2) // SLOTS)
                if j == 2:
                    down(0, 0, first=True)
            with pe.Fori(1, ROUNDS - 1) as i:
                for k in range(SLOTS):
                    j = i * SLOTS + k
                    up(j, k)
                    later_turn(j + 2, (k + 2) % SLOTS, i if k == 0 else i + 1)
                    down(j - 2, (k - 2) % SLOTS)
            for j in range(EXPERT_TILES - SLOTS, EXPERT_TILES + 2):
                if j < EXPERT_TILES:
                    up(j, j % SLOTS)
                if j + 2 < EXPERT_TILES:
                    later_turn(j + 2, (j + 2) % SLOTS, (j + 2) // SLOTS)
                down(j - 2, (j - 2) % SLOTS)
            shared_pair(1)

        @block.vector
        def _(dve):
            def norm_stats(src, b, stats_sem, var_sem):
                for n in range(b * TPB, (b + 1) * TPB):
                    ins = dve.bn_stats(stats[:, n, :], src[:, n, :])
                ins.then_inc(stats_sem, 1)
                dve.wait_ge(stats_sem, b + 1)
                for n in range(b * TPB, (b + 1) * TPB):
                    ins = dve.bn_aggr(mv[:, n, :], stats[:, n, :])
                ins.then_inc(var_sem, 1)

            def norm_apply(src, b, sd_sem, rstd_sem, y_sem):
                t = batch_tiles(b)
                dve.wait_ge(sd_sem, b + 1)
                dve.reciprocal(rstd[:, t], sd[:, t]).then_inc(rstd_sem, 1)
                dve.wait_ge(rstd_sem, b + 1)
                for n in range(b * TPB, (b + 1) * TPB):
                    ins = dve.tensor_scalar(y[:, n, :], src[:, n, :], mv[:, n, 0:1], rstd[:, n:n + 1],
                                            ALU.subtract, ALU.mult)
                    if y_sem is y_ready:
                        ins.then_inc(y_sem, 1)
                if y_sem is not y_ready:
                    ins.then_inc(y_sem, 1)

            for b in range(B):
                dve.wait_ge(x_in[b], 16)
                norm_stats(x_sb, b, stats_ready, var_ready)
            for b in range(B):
                norm_apply(x_sb, b, sd_ready, rstd_ready, y_ready)
            dve.wait_ge(aa_ready, B)
            for b in range(B):
                dve.wait_ge(d2_in_psum, b + 1)
                dve.tensor_scalar(dist[:, b, :], banks[4 + b][0:SMALL, :], aa[:, b:b + 1], 0.0, ALU.add, ALU.max
                                  ).then_inc(d2_ready, 1)

            dve.wait_ge(pads_ready, 1)
            dve.tensor_reduce(end_lane[:], ends[:], AX_X, ALU.max).then_inc(lanes_ready, 1)
            dve.wait_ge(lanes_ready, 1)
            dve.tensor_scalar(dsk[:, :, 0], best[:, :, 0], end_lane[:, 0:1], None, ALU.mult).then_inc(lanes_ready, 1)
            dve.tensor_scalar(cost[:, 0, 0:1], end_lane[:, 0:1], -BIG, BIG, ALU.mult, ALU.add
                              ).then_inc(lanes_ready, 1)
            dve.wait_ge(lanes_ready, 3)
            to_right = [min(lane + 1, 31) for lane in range(32)]
            to_left = [max(lane - 1, 0) for lane in range(32)]
            for s in range(STEPS):
                if s:
                    dve.wait_ge(cost_ready, s)
                dve.tensor_tensor(best[:, s, 1:W + 1], cost[:, s, 0:W], cost[:, s, 1:W + 1], ALU.min
                                  ).then_inc(best_ready, 1)
                dve.stream_shuffle(edge[:, s % 2:s % 2 + 1], cost[:, s, W:W + 1], to_right).then_inc(edge_ready, 1)
                if s % CHUNK == 0:
                    dve.wait_ge(dsk_in[s // CHUNK], 16 * B)
                dve.wait_ge(edge_ready, s + 1)
                dve.wait_ge(best_ready, s + 1)
                dve.tensor_tensor_scan(cost[:, s + 1, :], best[:, s, :], dsk[:, s, :], edge[:, s % 2:s % 2 + 1],
                                       ALU.min, ALU.add).then_inc(cost_ready, 1)
            dve.wait_ge(cost_ready, STEPS)
            came_left, came_up, came_diag = cost[:, 1:STEPS + 1, 0:W], cost[:, 0:STEPS, 1:W + 1], cost[:, 0:STEPS, 0:W]
            dve.tensor_tensor(left[:, :, 0:W], came_left, best[:, :, 1:W + 1], ALU.is_lt).then_inc(mask_ready, 1)
            dve.tensor_tensor(up, came_diag, came_up, ALU.is_gt).then_inc(mask_ready, 1)
            dve.tensor_tensor(leave[:, :, 0:W], came_left, best[:, :, 1:W + 1], ALU.is_ge).then_inc(mask_ready, 1)
            dve.memset(path[:, STEPS, :], 0.0).then_inc(mask_ready, 1)
            dve.memset(left[:, STEPS - 1, W:W + 1], 0.0).then_inc(mask_ready, 1)
            dve.memset(leave[:, STEPS - 1, W:W + 1], 0.0).then_inc(mask_ready, 1)
            dve.memset(inflow[:], 0.0).then_inc(mask_ready, 1)
            dve.wait_ge(mask_ready, 7)
            dve.scalar_tensor_tensor(leave[:, :, 0:W], up, 0.5, leave[:, :, 0:W], ALU.subtract, ALU.mult
                                     ).then_inc(mask_ready, 1)
            dve.tensor_scalar(left[:, :, W + 1], best[:, :, 0], 0.0, end_lane[:, 1:2], ALU.mult, ALU.is_equal
                              ).then_inc(mask_ready, 1)
            dve.stream_shuffle(left[:, 0:STEPS - 1, W], left[:, 1:STEPS, 0], to_left).then_inc(mask_ready, 1)
            dve.wait_ge(mask_ready, 10)
            dve.stream_shuffle(leave[:, 0:STEPS - 1, W], leave[:, 1:STEPS, 0], to_left).then_inc(mask_ready, 1)
            dve.tensor_copy(inflow[:, W - 1:W], end_lane[:, 1:2]).then_inc(inflow_ready, 1)
            dve.wait_ge(mask_ready, 11)
            for n, s in enumerate(reversed(range(STEPS))):
                if n:
                    dve.wait_ge(path_ready, n)
                    dve.scalar_tensor_tensor(sent[:], path[:, s + 1, :], 2.0, leave[:, s + 1, :], ALU.mult, ALU.mult
                                             ).then_inc(sent_ready, 1)
                dve.stream_shuffle(edge[:, s % 2:s % 2 + 1], path[:, s + 1, 0:1], to_left).then_inc(edge_ready, 1)
                if n:
                    dve.wait_ge(sent_ready, n)
                    dve.scalar_tensor_tensor(inflow[:, 0:W], sent[:, 1:W + 1], -1.0, sent[:, 0:W], ALU.is_equal, ALU.add
                                             ).then_inc(inflow_ready, 1)
                dve.wait_ge(edge_ready, STEPS + n + 1)
                dve.wait_ge(inflow_ready, n + 1)
                dve.tensor_tensor_scan(path[:, s, ::-1], left[:, s, W + 1:0:-1], inflow[:, ::-1],
                                       edge[:, s % 2:s % 2 + 1], ALU.mult, ALU.max).then_inc(path_ready, 1)

            for b in range(B):
                t = batch_tiles(b)
                dve.wait_ge(added_in_psum, b + 1)
                dve.tensor_tensor(x2[:, t, :].rearrange("p n d -> p (n d)"), banks[b][:],
                                  x_sb[:, t, :].rearrange("p n d -> p (n d)"), ALU.add).then_inc(x2_ready, 1)
                dve.wait_ge(x2_ready, b + 1)
                norm_stats(x2, b, stats2_ready, var2_ready)
            for b in range(B):
                norm_apply(x2, b, sd2_ready, rstd2_ready, y2_ready)
            for b in range(B):
                dve.wait_ge(y2T_hi_ready, b + 1)
                dve.tensor_tensor(yT_lo[:, b * S:(b + 1) * S], banks[4 + b][:], yT_hi[:, b * S:(b + 1) * S],
                                  ALU.subtract).then_inc(y2T_lo_ready, 1)

            def per_tile(v):
                return v.unsqueeze(2).to_broadcast([P, TILES, E])

            def per_expert(v):
                return v.unsqueeze(1).to_broadcast([P, TILES, E])

            def each_tile(v):
                return v.unsqueeze(2).to_broadcast([P, E, TILES])

            steps = [0]

            def routed(ins):
                steps[0] += 1
                ins.then_inc(route, 1)
                dve.wait_ge(route, steps[0])

            dve.wait_ge(logits_in_psum, 1)
            dve.scalar_tensor_tensor(logits[:], banks[0][:, 0:TILES * E].rearrange("p (n e) -> p n e", e=E),
                                     1.0 / WSCALE, per_expert(gate_b_sb[:]), ALU.mult, ALU.add).then_inc(logits_ready, 1)
            dve.wait_ge(score_ready, 1)
            for k, sc in enumerate((score, score2)):
                routed(dve.tensor_reduce(top[:, k, :], sc[:], AX_X, ALU.max))
                routed(dve.tensor_tensor(is_top[:], sc[:], per_tile(top[:, k, :]), ALU.is_equal))
                routed(dve.tensor_tensor(key[:], is_top[:], per_expert(rank_key[:]), ALU.mult))
                routed(dve.tensor_reduce(key_top[:], key[:], AX_X, ALU.max))
                routed(dve.tensor_tensor(pick[:, k], key[:], per_tile(key_top[:]), ALU.is_equal))
                if k == 0:
                    routed(dve.scalar_tensor_tensor(score2[:], pick[:, 0], -4.0, score[:], ALU.mult, ALU.add))
            dve.tensor_tensor(picked[:], pick[:, 0], pick[:, 1], ALU.add).then_inc(picked_ready, 1)
            routed(dve.scalar_tensor_tensor(denom[:], top[:, 0, :], 1e-6, top[:, 1, :], ALU.add, ALU.add))
            routed(dve.reciprocal(denom[:], denom[:]))
            for k in range(TOP):
                routed(dve.tensor_tensor(weight[:, k, :], top[:, k, :], denom[:], ALU.mult))
            dve.wait_ge(ranks_in_psum, 1)
            routed(dve.tensor_copy(in_tile[:], banks[5][:, 0:P].rearrange("p (n e) -> p e n", e=E)))
            routed(dve.tensor_tensor_scan(running[:].rearrange("p e n -> p (e n)"),
                                          carry_on[:].rearrange("p e n -> p (e n)"),
                                          in_tile[:].rearrange("p e n -> p (e n)"), 0.0, ALU.mult, ALU.add))
            routed(dve.tensor_tensor(exceeds[:], each_tile(running[:, :, TILES - 1]),
                                     thresholds[:].unsqueeze(1).to_broadcast([P, E, TILES]), ALU.is_gt))
            routed(dve.tensor_tensor(offset[:], running[:], in_tile[:], ALU.subtract))
            routed(dve.tensor_reduce(tiles_of[:], exceeds[:], AX_X, ALU.add))
            routed(dve.tensor_tensor_scan(tiles_upto[:], ones[:, 0:E], tiles_of[:], 0.0, ALU.mult, ALU.add))
            routed(dve.tensor_tensor(tiles_before[:], tiles_upto[:], tiles_of[:], ALU.subtract))
            routed(dve.scalar_tensor_tensor(offset[:], each_tile(tiles_before[:]), float(P), offset[:], ALU.mult, ALU.add))
            routed(dve.tensor_tensor(place[:], banks[4][:, 0:P].rearrange("p (n e) -> p n e", e=E),
                                     offset[:].rearrange("p e n -> p n e"), ALU.add))
            for k in range(TOP):
                routed(dve.tensor_tensor(part[:, k], pick[:, k], place[:], ALU.mult))
            routed(dve.tensor_reduce(slot_f[:], part[:], AX_X, ALU.add))
            dve.tensor_copy(slot[:], slot_f[:].rearrange("p k n -> p (k n)")).then_inc(slots_ready, 1)
            for k in range(TOP):
                routed(dve.scalar_tensor_tensor(part[:, k], pick[:, k], WSCALE, per_tile(weight[:, k, :]),
                                                ALU.mult, ALU.mult))
            dve.tensor_tensor(gates[:, :, 0:E], part[:, 0], part[:, 1], ALU.add).then_inc(gates_ready, 1)
            routed(dve.tensor_tensor(past[:], tiles_upto[0:1, :].unsqueeze(1).to_broadcast([1, EXPERT_TILES, E]),
                                     tile_no[:].unsqueeze(2).to_broadcast([1, EXPERT_TILES, E]), ALU.is_le))
            routed(dve.tensor_reduce(tile_expert_f[:], past[:], AX_X, ALU.add))
            dve.tensor_scalar(tile_expert[:], tile_expert_f[:], float(E - 1), None, ALU.min).then_inc(table_ready, 1)

            def shared_pair(q):
                for b in (2 * q, 2 * q + 1):
                    for c in range(NCH):
                        n = b * NCH + c
                        dve.wait_ge(s_gelu_done, n + 1)
                        if b >= 2:
                            dve.wait_ge(s_down_done, b - 1)
                        dve.tensor_copy(shared_hi[:, b % 2, c, :], shared_g[:, n % 2, :]).then_inc(s_hi_ready, 1)
                        dve.wait_ge(s_hi_ready, n + 1)
                        dve.tensor_tensor(shared_lo[:, b % 2, c, :], shared_g[:, n % 2, :], shared_hi[:, b % 2, c, :],
                                          ALU.subtract).then_inc(s_hid_ready, 1)
                for b in (2 * q, 2 * q + 1):
                    dve.wait_ge(s_down_done, b + 1)
                    dve.tensor_copy(acc[:, b * TPB * H:(b + 1) * TPB * H], banks[S_DOWN_BANK][:]).then_inc(acc_ready, 1)

            def x_low(j, k):
                dve.wait_ge(xT_hi_ready, j + 1)
                dve.tensor_tensor(xT_lo[:, k, :], banks[XT_BANK][:, 0:P], xT_hi[:, k, :], ALU.subtract
                                  ).then_inc(xT_ready, 1)

            def hidden_halves(j, k, first=False):
                dve.wait_ge(gelu_done, j + 1)
                if not first:
                    dve.wait_ge(y_done, j - 2)
                dve.tensor_copy(hid_hi[:, k, :], hid[:, k, :]).then_inc(hid_hi_ready, 1)
                dve.wait_ge(hid_hi_ready, j + 1)
                dve.tensor_tensor(hid_lo[:, k, :], hid[:, k, :], hid_hi[:, k, :], ALU.subtract).then_inc(hid_ready, 1)

            shared_pair(0)
            x_low(0, 0)
            x_low(1, 1)
            for j in range(SLOTS):
                hidden_halves(j, j, first=True)
                x_low(j + 2, (j + 2) % SLOTS)
            with dve.Fori(1, ROUNDS - 1) as i:
                for k in range(SLOTS):
                    hidden_halves(i * SLOTS + k, k)
                    x_low(i * SLOTS + (k + 2), (k + 2) % SLOTS)
            for j in range(EXPERT_TILES - SLOTS, EXPERT_TILES):
                hidden_halves(j, j % SLOTS)
                if j + 2 < EXPERT_TILES:
                    x_low(j + 2, (j + 2) % SLOTS)
            shared_pair(1)

            for b in range(B):
                tot, tsteps = total[:, b % 2], b * TOP * TPB
                dve.wait_ge(acc_ready, b + 1)
                dve.wait_ge(gather_in[b], 16 * TOP * TPB)
                for k in range(TOP):
                    if k:
                        dve.wait_ge(total_step, tsteps + k * TPB)
                    for n in range(TPB):
                        t = b * TPB + n
                        prev = tot[:, n, :] if k else acc[:, t * H:(t + 1) * H]
                        dve.scalar_tensor_tensor(tot[:, n, :], gathered[k][:, t * H:(t + 1) * H],
                                                 weight[:, k, t:t + 1], prev, ALU.mult, ALU.add).then_inc(total_step, 1)
                dve.wait_ge(total_step, tsteps + TOP * TPB)
                dve.tensor_reduce(peak[:, b, :], tot, AX_X, ALU.max, apply_absolute_value=True).then_inc(tail, 1)
                dve.wait_ge(tail, 4 * b + 1)
                dve.tensor_scalar(peak_eps[:, b, :], peak[:, b, :], OUT_SCALE / WSCALE, 1e-6, ALU.mult, ALU.add
                                  ).then_inc(tail, 1)
                dve.wait_ge(tail, 4 * b + 2)
                dve.reciprocal(peak[:, b, :], peak_eps[:, b, :]).then_inc(tail, 1)
                dve.wait_ge(tail, 4 * b + 3)
                dve.tensor_scalar(inv_peak[:, b, :], peak[:, b, :], OUT_SCALE / WSCALE, None, ALU.mult
                                  ).then_inc(tail, 1)
                dve.wait_ge(tail, 4 * b + 4)
                if b >= 2:
                    dve.wait_ge(out_done[b % 2], 16 * (b // 2))
                for n in range(TPB):
                    ins = dve.scalar_tensor_tensor(result[:, b % 2, n, :], tot[:, n, :], inv_peak[:, b, n:n + 1],
                                                   x2[:, b * TPB + n, :], ALU.mult, ALU.add)
                ins.then_inc(result_ready, 1)


_INS = ["x", "ctx_1024"] + ["L0_ffn_" + n for n in ("gate_w", "bias", "up_w", "up_b", "down_w", "down_b",
                                                   "sw_up", "sb_up", "sw_down", "sb_down")]


def kernel(**inputs):
    import numpy as np
    import concourse.bacc as bacc
    from concourse.bass_utils import run_bass_kernel_spmd

    nc = bacc.Bacc("TRN2", target_bir_lowering=False, num_devices=1)
    arrays, args = {}, []
    for name in _INS:
        a = np.ascontiguousarray(inputs[name])
        arrays[f"in_{name}"] = a
        args.append(nc.dram_tensor(f"in_{name}", a.shape, mybir.dt.from_np(a.dtype), kind="ExternalInput").ap())
    args.append(nc.dram_tensor("out_0", (B, S, H), F32, kind="ExternalOutput").ap())
    build(nc, *args)
    r = run_bass_kernel_spmd(nc, [arrays], core_ids=[0])
    return r.results[0]["out_0"]
```

```python
from contextlib import ExitStack

import concourse.bass as bass
from concourse import mybir

F32 = mybir.dt.float32
F16 = mybir.dt.float16
U32 = mybir.dt.uint32
ALU = mybir.AluOpType
ACT = mybir.ActivationFunctionType
AX_X = mybir.AxisListType.X

P = 128
B, S, H = 4, 512, 128
SMALL = 77
TILES = B * S // P
TPB = S // P
BLOCKS = 16
W = S // BLOCKS
STEPS = SMALL + BLOCKS - 1
LANES = B * BLOCKS
DIST_BOUNDS = 0, 8, 24, 48, STEPS
MASK_BOUNDS = 0, 24, 48, 66, 76, 84
MASK_STEPS = max(b - a for a, b in zip(MASK_BOUNDS, MASK_BOUNDS[1:]))
PATH_BOUNDS = STEPS, 64, 36, 8, 0
PAIRS = 2 * (W + 1)
PAD = BLOCKS - 1
PITCH = B * S
DRAM_ROWS = SMALL + 2 * PAD + (B - 1) * BLOCKS
BIG = 1e30
EPS = 1e-5
E, TOP = 8, 2
I = 4 * H
NCH = I // P
SLOTS = 2
S_SLOTS = 3
S_LAG = NCH + 2
UNROLL = 4
HALVES = 2
ET = 2 * P
PARTS = ET // P
TILES_EACH = B * S // ET
EXPERT_TILES = -(-((TOP * B * S + E * (ET - 1)) // ET) // SLOTS) * SLOTS
ROUNDS = EXPERT_TILES // SLOTS
WSCALE = 256.0
OUT_SCALE = 0.1


def build(nc, x, ctx_in, gate_w, gate_b, up_w, up_b, down_w, down_b, sw_up, sb_up, sw_down, sb_down, out):
    with ExitStack() as stack:
        def sb(name, shape, dt=F32):
            return stack.enter_context(nc.sbuf_tensor(name, shape, dt))

        def sem(name):
            return stack.enter_context(nc.semaphore(name))

        banks = [stack.enter_context(nc.psum_tensor(f"bank{i}", [P, 512], F32)) for i in range(8)]

        arena_a = sb("arena_a", [P, STEPS * (W + 1)])
        arena_b = sb("arena_b", [P, max((STEPS + 1) * (W + 1), S_SLOTS * NCH * S // 2)])
        arena_c = sb("arena_c", [P, STEPS * (W + 1)])
        arena_d = sb("arena_d", [P, STEPS * PAIRS])
        dsk = arena_a[0:LANES, :].rearrange("l (s w) -> l s w", w=W + 1)
        cost = arena_b[0:LANES, 0:(STEPS + 1) * (W + 1)].rearrange("l (s w) -> l s w", w=W + 1)
        best = arena_c[0:LANES, :].rearrange("l (s w) -> l s w", w=W + 1)
        arena_f = sb("arena_f", [P, STEPS * PAIRS])
        arena_g = sb("arena_g", [P, (STEPS + 1) * PAIRS])
        goes_on = arena_d[0:LANES, :].rearrange("l (s c) -> l s c", c=PAIRS)
        leaves = arena_f[0:LANES, :].rearrange("l (s c) -> l s c", c=PAIRS)
        path = arena_g[0:LANES, :].rearrange("l (s c) -> l s c", c=PAIRS)
        path_cells = arena_b[0:LANES, 0:STEPS * W].rearrange("l (s w) -> l s w", w=W)
        inflow = sb("inflow", [LANES, PAIRS])
        edge = sb("edge", [LANES, 2])
        ends = sb("ends", [LANES, 2, B])
        end_lane = sb("end_lane", [LANES, 2])
        big = sb("big", [PAD, S])

        x_sb = sb("x_sb", [P, TILES, H])
        ctx_sb = sb("ctx_sb", [SMALL, B, H])
        ident = sb("ident", [P, P])
        ones = sb("ones", [P, SMALL])
        eps = sb("eps", [P, 1])
        stats = sb("stats", [P, TILES, 6])
        mv = sb("mv", [P, TILES, 2])
        sd = sb("sd", [P, TILES])
        rstd = sb("rstd", [P, TILES])
        shift = sb("shift", [P, TILES])
        row_and_place = sb("row_and_place", [P, TILES, H + 2])
        y = row_and_place[:, :, 0:H]
        yT = arena_f[:, 0:B * S].rearrange("p (b s) -> p b s", s=S)
        ysqT = arena_f[:, B * S:2 * B * S].rearrange("p (b s) -> p b s", s=S)
        ctxm2T = sb("ctxm2T", [P, B, SMALL])
        ctxsq = sb("ctxsq", [SMALL, H])
        aa = sb("aa", [SMALL, B])
        dist = sb("dist", [SMALL, B, S])
        path_rows = dist
        x2 = sb("x2", [P, TILES, H])
        is_up = arena_g[0:LANES, 0:STEPS * W].rearrange("l (s w) -> l s w", w=W)
        stays = x2[0:LANES].rearrange("p n d -> p (n d)")[:, 0:MASK_STEPS * W].rearrange("l (s w) -> l s w", w=W)

        stage = sb("stage", [P, 2, I])
        up_hi = sb("up_hi", [P, (E + 1) * I], F16)
        up_lo = sb("up_lo", [P, (E + 1) * I], F16)
        down_hi = sb("down_hi", [P, (E + 1) * I], F16)
        down_lo = sb("down_lo", [P, (E + 1) * I], F16)
        gate_ld = sb("gate_ld", [P, E])
        gate_hi = sb("gate_hi", [P, E], F16)
        gate_lo = sb("gate_lo", [P, E], F16)
        gate_b_sb = sb("gate_b_sb", [P, E])
        bias_ld = sb("bias_ld", [(E + 1) * NCH, P])
        up_bias = sb("up_bias", [P, E + 1, NCH])
        tile_bias = sb("tile_bias", [P, EXPERT_TILES, NCH])
        down_b_all = sb("down_b_all", [E + 1, H])

        rank_key = sb("rank_key", [P, E])
        logits = sb("logits", [P, TILES, E])
        score = sb("score", [P, TILES, E])
        score2 = sb("score2", [P, TILES, E])
        top = sb("top", [P, TOP, TILES])
        is_top = sb("is_top", [P, TILES, E])
        key = sb("key", [P, TILES, E])
        key_top = sb("key_top", [P, TILES])
        pick = sb("pick", [P, TOP, TILES, E])
        picked = sb("picked", [P, TILES, E], F16)
        denom = sb("denom", [P, TILES])
        part = sb("part", [P, TOP, TILES, E])
        gates = sb("gates", [P, TILES, E + 1])
        before = sb("before", [P, P], F16)
        ones16 = sb("ones16", [P, P], F16)
        carry_on = sb("carry_on", [P, E, TILES])
        thresholds = sb("thresholds", [P, TILES_EACH])
        tile_no = sb("tile_no", [P, EXPERT_TILES])
        in_tile = sb("in_tile", [P, E, TILES])
        running = sb("running", [P, E, TILES])
        offset = sb("offset", [P, E, TILES])
        exceeds = sb("exceeds", [P, E, TILES_EACH])
        tiles_of = sb("tiles_of", [P, E])
        tiles_upto = sb("tiles_upto", [P, E])
        tiles_before = sb("tiles_before", [P, E])
        place = sb("place", [P, TILES, E])
        slot_f = sb("slot_f", [P, TOP, TILES])
        slot = sb("slot", [P, TOP * TILES], U32)
        past = sb("past", [P, EXPERT_TILES, E])
        started = sb("started", [P, EXPERT_TILES, E])
        tile_expert_f = sb("tile_expert_f", [1, EXPERT_TILES])
        tile_expert = sb("tile_expert", [1, EXPERT_TILES], U32)

        yT_hi = arena_a[:, 0:TILES * P // 2].bitcast(F16)
        yT_lo = arena_a[:, TILES * P // 2:TILES * P].bitcast(F16)
        by_token = arena_b[:, 0:TILES * H], arena_c[:, 0:TILES * H]
        acc = arena_d[:, 0:TILES * H]
        gatesT = ysqT[0:E + 1, :, :].rearrange("e b s -> e (b s)")

        def within(arena, start, shape, dt=F32):
            n = 1
            for m in shape:
                n *= m
            n = n // 2 if dt == F16 else n
            view = arena[:, start:start + n]
            view = view.bitcast(F16) if dt == F16 else view
            names = " ".join("abc"[:len(shape)])
            sizes = dict(zip("abc", shape))
            return view.rearrange(f"p ({names}) -> p {names}", **sizes), start + n

        x_flat = x_sb[:].rearrange("p n d -> p (n d)")
        total, at = within(x_flat, 0, (2, TPB, H))
        result, at = within(x_flat, at, (2, TPB, H))
        hid, at = within(arena_f, 0, (SLOTS, HALVES, I * PARTS // HALVES))
        hid_hi, at = within(arena_d, TILES * H, (SLOTS, HALVES, I * PARTS // HALVES), F16)
        shared_hi, _ = within(arena_b, 0, (S_SLOTS, NCH, S), F16)
        y_row, at = within(arena_d, at, (SLOTS, PARTS, H))
        xT_hi, at = within(arena_d, at, (SLOTS, ET), F16)
        xT_lo, at = within(arena_a, TILES * P, (SLOTS, ET), F16)
        hid_lo, at = within(arena_g, 0, (SLOTS, HALVES, I * PARTS // HALVES), F16)
        shared_g, at = within(arena_g, at, (2, S))
        shared_lo, at = within(arena_g, at, (S_SLOTS, NCH, S), F16)
        x_row, at = within(arena_g, at, (SLOTS, PARTS, H + 2))
        row_and_place2, at = within(arena_c, 0, (TILES, H + 2))
        weight = row_and_place[:, :, H + 1], row_and_place2[:, :, H + 1]
        zeros = sb("zeros", [P, H])
        pad_place = sb("pad_place", [P, EXPERT_TILES * PARTS, 2])
        result_weight = sb("result_weight", [P, EXPERT_TILES * PARTS])
        result_place = sb("result_place", [P, EXPERT_TILES * PARTS], U32)
        peak = sb("peak", [P, B, TPB])
        peak_eps = sb("peak_eps", [P, B, TPB])
        inv_peak = sb("inv_peak", [P, B, TPB])

        dist_dram = nc.dram_tensor("dist_dram", (DRAM_ROWS, PITCH), F32, kind="Internal")
        path_dram = nc.dram_tensor("path_dram", (DRAM_ROWS, PITCH), F32, kind="Internal")
        sorted_dram = nc.dram_tensor("sorted_dram", (EXPERT_TILES * ET, H + 2), F32, kind="Internal")
        expert_dram = nc.dram_tensor("expert_dram", (TOP * B * S + EXPERT_TILES * ET, H), F32, kind="Internal")

        x_in = [sem(f"x_in{b}") for b in range(B)]
        ctx_ld = sem("ctx_ld")
        small_ld = sem("small_ld")
        stage_ld = [sem(f"stage_ld{i}") for i in range(2)]
        const_ready = sem("const_ready")
        pads_ready = sem("pads_ready")
        big_ready = sem("big_ready")
        ffn_const_ready = sem("ffn_const_ready")
        pool_step = sem("pool_step")
        stats_ready = sem("stats_ready")
        var_ready = sem("var_ready")
        sd_ready = sem("sd_ready")
        rstd_ready = sem("rstd_ready")
        y_ready = sem("y_ready")
        yT_in_psum = sem("yT_in_psum")
        yT_ready = sem("yT_ready")
        ctxT_in_psum = sem("ctxT_in_psum")
        ctxT_ready = sem("ctxT_ready")
        aa_ready = sem("aa_ready")
        d2_in_psum = sem("d2_in_psum")
        d2_ready = sem("d2_ready")
        dist_ready = sem("dist_ready")
        pad_out = sem("pad_out")
        dist_out = sem("dist_out")
        dsk_in = [sem(f"dsk_in{k}") for k in range(len(DIST_BOUNDS) - 1)]
        lanes_ready = sem("lanes_ready")
        inputs_ready = sem("inputs_ready")
        back_inputs_ready = sem("back_inputs_ready")
        cost_ready = sem("cost_ready")
        mask_ready = sem("mask_ready")
        cells_ready = sem("cells_ready")
        marks_ready = sem("marks_ready")
        last_mask = sem("last_mask")
        compared = sem("compared")
        path_ready = sem("path_ready")
        path_out = sem("path_out")
        rows_in = [sem(f"rows_in{b}") for b in range(B)]
        added_in_psum = sem("added_in_psum")
        x2_ready = sem("x2_ready")
        scaled_ready = sem("scaled_ready")
        halves_hi = sem("halves_hi")
        halves_lo = sem("halves_lo")
        small_hi = sem("small_hi")
        biasT_in_psum = sem("biasT_in_psum")
        up_bias_ready = sem("up_bias_ready")
        tile_bias_ready = sem("tile_bias_ready")
        weights_ready = sem("weights_ready")
        stats2_ready = sem("stats2_ready")
        var2_ready = sem("var2_ready")
        sd2_ready = sem("sd2_ready")
        rstd2_ready = sem("rstd2_ready")
        shift_ready = sem("shift_ready")
        y2_ready = sem("y2_ready")
        y2T_in_psum = sem("y2T_in_psum")
        y2T_hi_ready = sem("y2T_hi_ready")
        y2T_lo_ready = sem("y2T_lo_ready")
        logits_in_psum = sem("logits_in_psum")
        logits_ready = sem("logits_ready")
        score_ready = sem("score_ready")
        route = sem("route")
        picked_ready = sem("picked_ready")
        ranks_in_psum = sem("ranks_in_psum")
        gates_ready = sem("gates_ready")
        gatesT_in_psum = sem("gatesT_in_psum")
        gatesT_ready = sem("gatesT_ready")
        slots_ready = sem("slots_ready")
        table_ready = sem("table_ready")
        zeroed = sem("zeroed")
        scattered = sem("scattered")
        second_rows = sem("second_rows")
        place_kept = sem("place_kept")
        x_row_in = [sem(f"x_row_in{k}") for k in range(SLOTS)]
        xT_in_psum = sem("xT_in_psum")
        xT_hi_ready = sem("xT_hi_ready")
        xT_ready = sem("xT_ready")
        up_done = sem("up_done")
        gelu_done = sem("gelu_done")
        hid_hi_ready = sem("hid_hi_ready")
        hid_ready = sem("hid_ready")
        y_done = sem("y_done")
        y_row_ready = sem("y_row_ready")
        y_row_out = [sem(f"y_row_out{k}") for k in range(SLOTS)]
        s_up_done = sem("s_up_done")
        s_gelu_done = sem("s_gelu_done")
        s_hi_ready = sem("s_hi_ready")
        s_hid_ready = sem("s_hid_ready")
        s_down_done = sem("s_down_done")
        acc_ready = sem("acc_ready")
        by_token_in = [sem(f"by_token_in{b}") for b in range(B)]
        pair_ready = sem("pair_ready")
        tail = sem("tail")
        result_ready = sem("result_ready")
        out_done = [sem(f"out_done{i}") for i in range(2)]

        x_tiles = x.rearrange("b (n p) d -> b p n d", p=P)
        out_tiles = out.rearrange("b (n p) d -> b p n d", p=P)
        UP_BANK = 0
        XT_BANKS = 4, 7
        S_DOWN_BANKS = 7, 5
        S_UP_BANKS = 6, 3
        Y_BANKS = 5, 6

        def batch_tiles(b):
            return slice(b * TPB, (b + 1) * TPB)

        def skewed(dram, s0, s1):
            return bass.AP(tensor=dram, offset=(PAD + s0 - (BLOCKS - 1)) * PITCH + B * S - W,
                           ap=[[PITCH - W, LANES], [PITCH, s1 - s0], [1, W]])

        def matrix_rows(dram, r0, r1, b0=0, b1=B):
            return bass.AP(tensor=dram, offset=(PAD + r0 + BLOCKS * b0) * PITCH + (B - 1 - b0) * S,
                           ap=[[PITCH, r1 - r0], [BLOCKS * PITCH - S, b1 - b0], [1, S]])

        def mask_views(s0, s1):
            odd, even = slice(2 * W + 1, 1, -2), slice(2 * W, 0, -2)
            return goes_on[:, s0:s1, odd], leaves[:, s0:s1, even], leaves[:, s0:s1, odd]

        block = stack.enter_context(nc.Block())

        @block.sync
        def _(sp):
            for b in range(B):
                sp.dma_start(x_sb[:, batch_tiles(b), :], x_tiles[b]).then_inc(x_in[b], 16)
            sp.wait_ge(big_ready, 1)
            for r0 in (-PAD, SMALL):
                sp.dma_start(matrix_rows(dist_dram, r0, r0 + PAD), big[:].unsqueeze(1).to_broadcast([PAD, B, S])
                             ).then_inc(pad_out, 16)
            for b in range(B):
                sp.wait_ge(dist_ready, b + 1)
                sp.dma_start(matrix_rows(dist_dram, 0, SMALL, b, b + 1), dist[:, b:b + 1, :]).then_inc(dist_out, 16)
            sp.wait_ge(pad_out, 16 * 2)
            sp.wait_ge(dist_out, 16 * B)
            for k, (s0, s1) in enumerate(zip(DIST_BOUNDS, DIST_BOUNDS[1:])):
                sp.dma_start(dsk[:, s0:s1, 1:W + 1], skewed(dist_dram, s0, s1)).then_inc(dsk_in[k], 16)
            sp.dma_start(bias_ld[0:E * NCH, :], up_b.rearrange("e (c p) -> (e c) p", p=P)).then_inc(small_ld, 16)
            sp.dma_start(bias_ld[E * NCH:(E + 1) * NCH, :], sb_up.rearrange("(c p) -> c p", p=P)
                         ).then_inc(small_ld, 16)
            sp.dma_start(gate_ld[:], gate_w).then_inc(small_ld, 16)
            sp.dma_start(gate_b_sb[:], gate_b.partition_broadcast(P)).then_inc(small_ld, 16)
            sp.dma_start(down_b_all[0:E, :], down_b).then_inc(small_ld, 16)
            sp.dma_start(down_b_all[E:E + 1, :], sb_down.rearrange("(a d) -> a d", a=1)).then_inc(small_ld, 16)
            sp.wait_ge(ffn_const_ready, 1)
            pads = sorted_dram.ap().rearrange("(j p) d -> p j d", p=P)
            with nc.allow_non_contiguous_dma(reason="two numbers a row, while the warping runs"):
                sp.dma_start(pads[:, :, H:H + 2], pad_place[:]).then_inc(zeroed, 16)
            sp.dma_start(pads[:, :, 0:H], zeros[:].unsqueeze(1).to_broadcast([P, EXPERT_TILES * PARTS, H])).then_inc(zeroed, 16)
            for e in range(E + 1):
                for m in range(2):
                    n = 2 * e + m
                    if n >= 2:
                        sp.wait_ge(halves_lo, n - 1)
                    if m == 0:
                        sp.dma_start(stage[:, 0, :], up_w[e] if e < E else sw_up).then_inc(stage_ld[0], 16)
                    else:
                        src = down_w[e] if e < E else sw_down
                        sp.dma_start(stage[:, 1, :].rearrange("p (c d) -> p c d", d=H),
                                     src.rearrange("(c p) d -> p c d", p=P)).then_inc(stage_ld[1], 16)
            for k, (s1, s0) in enumerate(zip(PATH_BOUNDS, PATH_BOUNDS[1:])):
                sp.wait_ge(cells_ready, k + 1)
                sp.dma_start(skewed(path_dram, s0, s1), path_cells[:, s0:s1, :]).then_inc(path_out, 16)
            sp.wait_ge(path_out, 16 * (len(PATH_BOUNDS) - 1))
            for b in range(B):
                sp.dma_start(path_rows[:, b:b + 1, :], matrix_rows(path_dram, 0, SMALL, b, b + 1)).then_inc(rows_in[b], 16)

            def load(j, k):
                rows = sorted_dram.ap()[bass.ds(j * ET, ET), :].rearrange("(n p) d -> p n d", p=P)
                sp.dma_start(x_row[:, k], rows).then_inc(x_row_in[k], 16)

            sp.wait_ge(scattered, 16 * TOP * TILES)
            for k in range(SLOTS):
                load(k, k)
            with sp.Fori(0, ROUNDS - 1) as i:
                for k in range(SLOTS):
                    sp.wait_ge(xT_in_psum, i * SLOTS + (k + 1))
                    sp.wait_ge(place_kept, i * SLOTS + (k + 1))
                    load(i * SLOTS + (k + SLOTS), k)
            for k in range(SLOTS):
                sp.wait_ge(y_row_out[k], 16 * PARTS * ROUNDS)
            for b in range(B):
                for k in range(TOP):
                    first = k * B * S + b * S
                    sp.dma_start(by_token[k][:, b * S:(b + 1) * S].rearrange("p (n d) -> p n d", d=H),
                                 expert_dram.ap()[first:first + S, :].rearrange("(n p) d -> p n d", p=P)
                                 ).then_inc(by_token_in[b], 16)
            for b in range(B):
                sp.wait_ge(result_ready, b + 1)
                sp.dma_start(out_tiles[b], result[:, b % 2, :, :]).then_inc(out_done[b % 2], 16)
            for i in range(2):
                sp.wait_ge(out_done[i], 16 * B // 2)

        @block.gpsimd
        def _(pool):
            pool.memset(ident[:], 0.0).then_inc(pool_step, 1)
            pool.memset(ones[:], 1.0)
            pool.memset(eps[:], EPS)
            pool.wait_ge(pool_step, 1)
            pool.affine_select(out=ident[:], in_=ident[:], compare_op=ALU.not_equal, fill=1.0, base=0,
                               pattern=[[-1, P]], channel_multiplier=1).then_inc(const_ready, 1)
            pool.memset(big[:], BIG).then_inc(big_ready, 1)
            pool.memset(best[:, :, 0], BIG)
            pool.memset(cost[:, 0, :], BIG)
            pool.memset(ends[:], 0.0).then_inc(pool_step, 1)
            pool.wait_ge(pool_step, 2)
            for e in range(2):
                last = pool.affine_select(out=ends[:, e, :], in_=ends[:, e, :], compare_op=ALU.not_equal, fill=1.0,
                                          base=(e - 1) * (BLOCKS - 1), pattern=[[-BLOCKS, B]], channel_multiplier=1)
            last.then_inc(pads_ready, 1)
            pool.memset(goes_on[:, :, 2::2], 1.0)
            pool.memset(path[:, STEPS, :], 0.0)
            pool.memset(inflow[:], 0.0)
            pool.memset(goes_on[:, STEPS - 1, 1:2], 0.0).then_inc(marks_ready, 1)
            for e in range(E):
                pool.memset(rank_key[:, e:e + 1], float(E - e))
            pool.memset(gates[:, :, E], WSCALE)
            pool.memset(zeros[:], 0.0)
            pool.memset(before[:], 1.0)
            pool.memset(ones16[:], 1.0)
            pool.memset(carry_on[:], 1.0)
            pool.iota(thresholds[:], pattern=[[ET, TILES_EACH]], base=0, channel_multiplier=0,
                      allow_small_or_imprecise_dtypes=True)
            pool.iota(row_and_place[:, :, H], pattern=[[P, TILES]], base=0, channel_multiplier=1,
                      allow_small_or_imprecise_dtypes=True)
            pool.memset(pad_place[:, :, 1], 0.0)
            pool.iota(pad_place[:, :, 0], pattern=[[P, EXPERT_TILES * PARTS]], base=TOP * B * S, channel_multiplier=1,
                      allow_small_or_imprecise_dtypes=True)
            pool.iota(tile_no[:], pattern=[[1, EXPERT_TILES]], base=0, channel_multiplier=0,
                      allow_small_or_imprecise_dtypes=True).then_inc(pool_step, 1)
            pool.wait_ge(pool_step, 3)
            pool.memset(carry_on[:, :, 0], 0.0)
            pool.affine_select(out=before[:], in_=before[:], compare_op=ALU.is_ge, fill=0.0, base=-1,
                               pattern=[[1, P]], channel_multiplier=-1).then_inc(ffn_const_ready, 1)
            pool.wait_ge(compared, 1)
            pool.memset(leaves[:, :, 0], 0.0)
            pool.memset(leaves[:, STEPS - 1, 1:2], 0.0).then_inc(marks_ready, 1)
            for k, (s0, s1) in enumerate(zip(MASK_BOUNDS, MASK_BOUNDS[1:])):
                went_left, went_up, went_diag = mask_views(s0, s1)
                not_left = stays[:, 0:s1 - s0, :]
                if k:
                    pool.wait_ge(mask_ready, 3 * k)
                pool.wait_ge(compared, s1)
                pool.tensor_scalar(not_left, went_left, -1.0, 1.0, ALU.mult, ALU.add).then_inc(mask_ready, 1)
                pool.wait_ge(mask_ready, 3 * k + 1)
                pool.tensor_tensor(went_up, is_up[:, s0:s1], not_left, ALU.mult).then_inc(mask_ready, 1)
                pool.wait_ge(mask_ready, 3 * k + 2)
                pool.tensor_tensor(went_diag, not_left, went_up, ALU.subtract).then_inc(mask_ready, 1)
            pool.wait_ge(small_hi, 1)
            pool.tensor_tensor(gate_lo[:], gate_ld[:], gate_hi[:], ALU.subtract).then_inc(weights_ready, 1)
            for e in range(E + 1):
                cols = slice(e * I, (e + 1) * I)
                for m, (hi, lo) in enumerate(((up_hi, up_lo), (down_hi, down_lo))):
                    pool.wait_ge(halves_hi, 2 * e + m + 1)
                    pool.tensor_tensor(lo[:, cols], stage[:, m, :], hi[:, cols], ALU.subtract).then_inc(halves_lo, 1)
            pool.wait_ge(path_out, 16 * (len(PATH_BOUNDS) - 1))
            pool.iota(row_and_place2[:, :, H], pattern=[[P, TILES]], base=B * S, channel_multiplier=1,
                      allow_small_or_imprecise_dtypes=True).then_inc(second_rows, 1)
            for b in range(B):
                pool.wait_ge(y2_ready, b + 1)
                pool.tensor_copy(row_and_place2[:, batch_tiles(b), 0:H], y[:, batch_tiles(b), :]
                                 ).then_inc(second_rows, 1)
            pool.wait_ge(zeroed, 16 * 2)
            pool.wait_ge(slots_ready, 1)
            for k, src in enumerate((row_and_place, row_and_place2)):
                if k:
                    pool.wait_ge(second_rows, 1 + B)
                for t in range(TILES):
                    pool.indirect_dma_start(
                        out=sorted_dram.ap(), in_=src[:, t, :], in_offset=None,
                        out_offset=bass.IndirectOffsetOnAxis(ap=slot[:, k * TILES + t:k * TILES + t + 1], axis=0)
                    ).then_inc(scattered, 16)

            def keep_place(j):
                pool.wait_ge(x_row_in[j % SLOTS], 16 * (j // SLOTS + 1))
                pool.tensor_copy(result_weight[:, j * PARTS:(j + 1) * PARTS], x_row[:, j % SLOTS, :, H + 1])
                pool.tensor_copy(result_place[:, j * PARTS:(j + 1) * PARTS], x_row[:, j % SLOTS, :, H]
                                 ).then_inc(place_kept, 1)

            ahead = 2 * SLOTS
            for j in range(ahead):
                keep_place(j)
            for j in range(EXPERT_TILES):
                if j + ahead < EXPERT_TILES:
                    keep_place(j + ahead)
                pool.wait_ge(place_kept, j + 1)
                pool.wait_ge(y_row_ready, j + 1)
                for n in range(PARTS):
                    place_of = result_place[:, j * PARTS + n:j * PARTS + n + 1]
                    pool.indirect_dma_start(
                        out=expert_dram.ap(), in_=y_row[:, j % SLOTS, n, :], in_offset=None,
                        out_offset=bass.IndirectOffsetOnAxis(ap=place_of, axis=0)
                    ).then_inc(y_row_out[j % SLOTS], 16)
            for b in range(B):
                cols = slice(b * S, (b + 1) * S)
                pool.wait_ge(by_token_in[b], 16 * TOP)
                pool.tensor_tensor(by_token[0][:, cols], by_token[0][:, cols], by_token[1][:, cols], ALU.add
                                   ).then_inc(pair_ready, 1)

        @block.scalar
        def _(act):
            act.dma_start(ctx_sb[:], ctx_in.rearrange("b i d -> i b d")).then_inc(ctx_ld, 16)
            act.wait_ge(ctx_ld, 16)
            for b in range(B):
                act.activation(ctxsq[:], ctx_sb[:, b, :], ACT.Square, accum_out=aa[:, b:b + 1]).then_inc(aa_ready, 1)
                act.wait_ge(aa_ready, b + 1)
            act.wait_ge(ctxT_in_psum, 1)
            act.mul(ctxm2T[:].rearrange("p b i -> p (b i)"), banks[7][:, 0:B * SMALL], -2.0).then_inc(ctxT_ready, 1)
            act.wait_ge(const_ready, 1)
            for b in range(B + 1):
                if b < B:
                    t = batch_tiles(b)
                    act.wait_ge(var_ready, b + 1)
                    act.activation(sd[:, t], mv[:, t, 1], ACT.Sqrt, bias=eps[:]).then_inc(sd_ready, 1)
                if b:
                    act.wait_ge(yT_in_psum, b)
                    act.activation(yT[:, b - 1, :], banks[b - 1][:], ACT.Copy).then_inc(yT_ready, 1)
                    act.activation(ysqT[:, b - 1, :], banks[b - 1][:], ACT.Square).then_inc(yT_ready, 1)
            for b in range(B):
                act.wait_ge(d2_ready, b + 1)
                act.activation(dist[:, b, :], dist[:, b, :], ACT.Sqrt).then_inc(dist_ready, 1)
            act.wait_ge(small_ld, 16 * 6)
            act.mul(gate_ld[:], gate_ld[:], WSCALE).then_inc(scaled_ready, 1)
            act.wait_ge(biasT_in_psum, 1)
            act.activation(up_bias[:].rearrange("p e c -> p (e c)"), banks[0][:, 0:(E + 1) * NCH], ACT.Copy
                           ).then_inc(up_bias_ready, 1)
            act.wait_ge(scaled_ready, 1)
            act.activation(gate_hi[:], gate_ld[:], ACT.Copy).then_inc(small_hi, 1)
            for e in range(E + 1):
                cols = slice(e * I, (e + 1) * I)
                for m, hi in enumerate((up_hi, down_hi)):
                    n = 2 * e + m
                    act.wait_ge(stage_ld[m], 16 * (e + 1))
                    act.mul(stage[:, m, :], stage[:, m, :], WSCALE).then_inc(scaled_ready, 1)
                    act.wait_ge(scaled_ready, n + 2)
                    act.activation(hi[:, cols], stage[:, m, :], ACT.Copy).then_inc(halves_hi, 1)
            for s1, s0 in zip(PATH_BOUNDS, PATH_BOUNDS[1:]):
                act.wait_ge(path_ready, STEPS - s0)
                act.activation(path_cells[:, s0:s1, :], path[:, s0:s1, 2 * W:0:-2], ACT.Copy).then_inc(cells_ready, 1)
            for b in range(B + 2):
                if b < B:
                    t = batch_tiles(b)
                    act.wait_ge(var2_ready, b + 1)
                    act.activation(sd[:, t], mv[:, t, 1], ACT.Sqrt, bias=eps[:]).then_inc(sd2_ready, 1)
                if 0 < b <= B:
                    act.wait_ge(shift_ready, b)
                    for t in range((b - 1) * TPB, b * TPB):
                        last = act.activation(y[:, t, :], x2[:, t, :], ACT.Identity, bias=shift[:, t:t + 1],
                                              scale=rstd[:, t:t + 1])
                    last.then_inc(y2_ready, 1)
                if b > 1:
                    act.wait_ge(y2T_in_psum, b - 1)
                    act.activation(yT_hi[:, (b - 2) * S:(b - 1) * S], banks[4 + b - 2][:], ACT.Copy
                                   ).then_inc(y2T_hi_ready, 1)
            act.wait_ge(logits_ready, 1)
            act.activation(score[:], logits[:], ACT.Sigmoid).then_inc(score_ready, 1)
            act.wait_ge(gatesT_in_psum, 1)
            for b in range(B):
                act.activation(gatesT[:, b * S:(b + 1) * S], banks[b][0:E + 1, :], ACT.Copy).then_inc(gatesT_ready, 1)

            def shared():
                for n in range(B * NCH):
                    act.wait_ge(s_up_done, n + 1)
                    if n >= 2:
                        act.wait_ge(s_hid_ready, n - 1)
                    act.activation(shared_g[:, n % 2, :], banks[S_UP_BANKS[n % 2]][:], ACT.Gelu,
                                   bias=up_bias[:, E, n % NCH:n % NCH + 1], scale=1.0 / WSCALE).then_inc(s_gelu_done, 1)

            def x_high(j, k):
                act.wait_ge(xT_in_psum, j + 1)
                act.activation(xT_hi[:, k, :], banks[XT_BANKS[k]][:, 0:ET], ACT.Copy).then_inc(xT_hi_ready, 1)

            def gelu(j, k, first=False):
                for m in range(HALVES):
                    act.wait_ge(up_done, j * HALVES + (m + 1))
                    if not first:
                        act.wait_ge(hid_ready, j * HALVES + (m + 1 - SLOTS * HALVES))
                    for q in range(NCH // HALVES):
                        cols = slice(q * ET, (q + 1) * ET)
                        bias = tile_bias[:, bass.ds(j, 1), m * (NCH // HALVES) + q]
                        last = act.activation(hid[:, k, m, cols], banks[UP_BANK + HALVES * k + m][:, cols], ACT.Gelu,
                                              bias=bias, scale=1.0 / WSCALE)
                    last.then_inc(gelu_done, 1)

            def y_copy(j, k, i, first=False):
                act.wait_ge(y_done, j + 1)
                if not first:
                    act.wait_ge(y_row_out[k], i * (16 * PARTS))
                for n in range(PARTS):
                    last = act.activation(y_row[:, k, n], banks[Y_BANKS[k]][:, n * H:(n + 1) * H], ACT.Copy,
                                          scale=result_weight[:, bass.ds(j * PARTS + n, 1)])
                last.then_inc(y_row_ready, 1)

            shared()
            for k in range(SLOTS):
                x_high(k, k)
            act.wait_ge(tile_bias_ready, NCH)
            for k in range(SLOTS):
                gelu(k, k, first=True)
                x_high(k + SLOTS, k)
            for k in range(SLOTS):
                y_copy(k, k, 0, first=True)
                gelu(SLOTS + k, k)
                x_high(2 * SLOTS + k, k)
            with act.Fori(2, ROUNDS - 1) as i:
                for k in range(SLOTS):
                    j = i * SLOTS + k
                    y_copy(j - SLOTS, k, i - 1)
                    gelu(j, k)
                    x_high(j + SLOTS, k)
            for k in range(SLOTS):
                j = EXPERT_TILES - SLOTS + k
                y_copy(j - SLOTS, k, ROUNDS - 2)
                gelu(j, k)
            act.wait_ge(place_kept, EXPERT_TILES)
            for k in range(SLOTS):
                y_copy(EXPERT_TILES - SLOTS + k, k, ROUNDS - 1)

        @block.tensor
        def _(pe):
            pe.wait_ge(const_ready, 1)
            pe.wait_ge(ctx_ld, 16)
            for b in range(B):
                mm = pe.transpose(banks[7][:, b * SMALL:(b + 1) * SMALL], ctx_sb[:, b, :], ident[0:SMALL, 0:SMALL])
            mm.then_inc(ctxT_in_psum, 1)
            for b in range(B + 1):
                if b < B:
                    for n in range(TPB):
                        pe.wait_ge(y_ready, b * TPB + n + 1)
                        mm = pe.transpose(banks[b][:, n * P:(n + 1) * P], y[:, b * TPB + n, :], ident[:])
                    mm.then_inc(yT_in_psum, 1)
                if b:
                    if b == 1:
                        pe.wait_ge(ctxT_ready, 1)
                    pe.wait_ge(yT_ready, 2 * b - 1)
                    pe.matmul(banks[3 + b][0:SMALL, :], ctxm2T[:, b - 1, :], yT[:, b - 1, :], start=True, stop=False)
                    pe.wait_ge(yT_ready, 2 * b)
                    pe.matmul(banks[3 + b][0:SMALL, :], ones[:], ysqT[:, b - 1, :], start=False, stop=True
                              ).then_inc(d2_in_psum, 1)
            pe.wait_ge(small_ld, 16 * 6)
            pe.transpose(banks[0][:, 0:(E + 1) * NCH], bias_ld[:], ident[0:(E + 1) * NCH, 0:(E + 1) * NCH]
                         ).then_inc(biasT_in_psum, 1)
            for b in range(B):
                pe.wait_ge(rows_in[b], 16)
                for n in range(TPB):
                    mm = pe.matmul(banks[b][:, n * P:(n + 1) * P], path_rows[:, b, n * P:(n + 1) * P],
                                   ctx_sb[:, b, :], start=True, stop=True)
                mm.then_inc(added_in_psum, 1)
            for b in range(B):
                pe.wait_ge(y2_ready, b + 1)
                for n in range(TPB):
                    mm = pe.transpose(banks[4 + b][:, n * P:(n + 1) * P], y[:, b * TPB + n, :], ident[:])
                mm.then_inc(y2T_in_psum, 1)
            pe.wait_ge(weights_ready, 1)
            pe.wait_ge(x2_ready, B)
            for t in range(TILES):
                cols = slice(t * P, (t + 1) * P)
                if t % TPB == 0:
                    pe.wait_ge(y2T_lo_ready, t // TPB + 1)
                o = banks[0][:, t * E:(t + 1) * E]
                pe.matmul(o, yT_hi[:, cols], gate_hi[:], start=True, stop=False)
                pe.matmul(o, yT_hi[:, cols], gate_lo[:], start=False, stop=False)
                mm = pe.matmul(o, yT_lo[:, cols], gate_hi[:], start=False, stop=True)
            mm.then_inc(logits_in_psum, 1)
            pe.wait_ge(picked_ready, 1)
            chosen = picked[:].rearrange("p n e -> p (n e)")
            pe.matmul(banks[4][:, 0:P], before[:], chosen, start=True, stop=True)
            pe.matmul(banks[5][:, 0:P], ones16[:], chosen, start=True, stop=True).then_inc(ranks_in_psum, 1)
            pe.wait_ge(gates_ready, 1)
            for t in range(TILES):
                mm = pe.transpose(banks[t // TPB][0:E + 1, t % TPB * P:(t % TPB + 1) * P], gates[:, t, :], ident[:])
            mm.then_inc(gatesT_in_psum, 1)
            pe.wait_ge(halves_lo, 2 * (E + 1))
            pe.wait_ge(slots_ready, 1)

            def three_passes(o, a_hi, a_lo, b_hi, b_lo, start, stop):
                pe.matmul(o, a_hi, b_hi, start=start, stop=False)
                pe.matmul(o, a_hi, b_lo, start=False, stop=False)
                return pe.matmul(o, a_lo, b_hi, start=False, stop=stop)

            def shared_up(b, c):
                n = b * NCH + c
                if n == 1:
                    pe.wait_ge(gatesT_ready, B)
                if n >= 2:
                    pe.wait_ge(s_gelu_done, n - 1)
                w = slice(E * I + c * P, E * I + (c + 1) * P)
                t = slice(b * S, (b + 1) * S)
                three_passes(banks[S_UP_BANKS[n % 2]][:], up_hi[:, w], up_lo[:, w], yT_hi[:, t], yT_lo[:, t],
                             True, True).then_inc(s_up_done, 1)

            def shared_down(b, n):
                if n == 0:
                    pe.wait_ge(s_hid_ready, (b + 1) * NCH)
                    if b > 1:
                        pe.wait_ge(acc_ready, b - 1)
                o = banks[S_DOWN_BANKS[b % 2]][:, n * H:(n + 1) * H]
                t = b * TPB + n
                pe.matmul(o, gatesT[:, t * P:(t + 1) * P], down_b_all[:], start=True, stop=False)
                for c in range(NCH):
                    w = slice(E * I + c * P, E * I + (c + 1) * P)
                    h = slice(n * P, (n + 1) * P)
                    mm = three_passes(o, shared_hi[:, b % S_SLOTS, c, h], shared_lo[:, b % S_SLOTS, c, h],
                                      down_hi[:, w], down_lo[:, w], False, c == NCH - 1)
                if n == TPB - 1:
                    mm.then_inc(s_down_done, 1)

            def shared():
                for m in range(B * NCH + S_LAG):
                    if m < B * NCH:
                        shared_up(m // NCH, m % NCH)
                    if m >= S_LAG:
                        shared_down((m - S_LAG) // TPB, (m - S_LAG) % TPB)

            expert_reg = [pe.alloc_register(f"expert{k}") for k in range(SLOTS)]

            def turn(j, k, r):
                pe.wait_ge(x_row_in[k], (r + 1) * 16)
                for n in range(PARTS):
                    mm = pe.transpose(banks[XT_BANKS[k]][:, n * P:(n + 1) * P], x_row[:, k, n, 0:H], ident[:])
                mm.then_inc(xT_in_psum, 1)

            def up(j, k):
                pe.reg_load(expert_reg[k], tile_expert[0:1, bass.ds(j, 1)])
                e = pe.snap(expert_reg[k], min_val=0, max_val=E - 1)
                pe.wait_ge(xT_ready, j + 1)
                for m in range(HALVES):
                    for q in range(NCH // HALVES):
                        c = m * (NCH // HALVES) + q
                        o = banks[UP_BANK + HALVES * k + m][:, q * ET:(q + 1) * ET]
                        w = bass.ds(e * I + c * P, P)
                        mm = three_passes(o, up_hi[:, w], up_lo[:, w], xT_hi[:, k, :], xT_lo[:, k, :], True, True)
                    mm.then_inc(up_done, 1)

            def down(j, k):
                e = pe.snap(expert_reg[k], min_val=0, max_val=E - 1)
                pe.wait_ge(hid_ready, j * HALVES + HALVES)
                for n in range(PARTS):
                    for c in range(NCH):
                        w = bass.ds(e * I + c * P, P)
                        m, q = c // (NCH // HALVES), c % (NCH // HALVES)
                        h = slice(q * ET + n * P, q * ET + (n + 1) * P)
                        mm = three_passes(banks[Y_BANKS[k]][:, n * H:(n + 1) * H], hid_hi[:, k, m, h], hid_lo[:, k, m, h],
                                          down_hi[:, w], down_lo[:, w], c == 0, c == NCH - 1)
                mm.then_inc(y_done, 1)

            shared()
            pe.wait_ge(table_ready, 1)
            pe.wait_ge(acc_ready, B)
            for k in range(SLOTS):
                turn(k, k, 0)
            for k in range(SLOTS):
                up(k, k)
                turn(SLOTS + k, k, 1)
            with pe.Fori(0, (EXPERT_TILES - 2 * SLOTS) // UNROLL) as i:
                for u in range(UNROLL):
                    j, k = i * UNROLL + (SLOTS + u), u % SLOTS
                    down(j - SLOTS, k)
                    up(j, k)
                    turn(j + SLOTS, k, i * (UNROLL // SLOTS) + (2 + u // SLOTS))
            for k in range(SLOTS):
                down(EXPERT_TILES - 2 * SLOTS + k, k)
                up(EXPERT_TILES - SLOTS + k, k)
            for k in range(SLOTS):
                down(EXPERT_TILES - SLOTS + k, k)

        @block.vector
        def _(dve):
            def norm_stats(src, b, stats_sem, var_sem):
                for n in range(b * TPB, (b + 1) * TPB):
                    ins = dve.bn_stats(stats[:, n, :], src[:, n, :])
                ins.then_inc(stats_sem, 1)
                dve.wait_ge(stats_sem, b + 1)
                for n in range(b * TPB, (b + 1) * TPB):
                    ins = dve.bn_aggr(mv[:, n, :], stats[:, n, :])
                ins.then_inc(var_sem, 1)

            def norm_apply(src, b, sd_sem, rstd_sem, y_sem):
                t = batch_tiles(b)
                dve.wait_ge(sd_sem, b + 1)
                dve.reciprocal(rstd[:, t], sd[:, t]).then_inc(rstd_sem, 1)
                dve.wait_ge(rstd_sem, b + 1)
                for n in range(b * TPB, (b + 1) * TPB):
                    ins = dve.tensor_scalar(y[:, n, :], src[:, n, :], mv[:, n, 0:1], rstd[:, n:n + 1],
                                            ALU.subtract, ALU.mult)
                    if y_sem is y_ready:
                        ins.then_inc(y_sem, 1)
                if y_sem is not y_ready:
                    ins.then_inc(y_sem, 1)

            for b in range(B + 1):
                if b < B:
                    dve.wait_ge(x_in[b], 16)
                    norm_stats(x_sb, b, stats_ready, var_ready)
                if b:
                    norm_apply(x_sb, b - 1, sd_ready, rstd_ready, y_ready)
            dve.wait_ge(aa_ready, B)
            for b in range(B):
                dve.wait_ge(d2_in_psum, b + 1)
                dve.tensor_scalar(dist[:, b, :], banks[4 + b][0:SMALL, :], aa[:, b:b + 1], 0.0, ALU.add, ALU.max
                                  ).then_inc(d2_ready, 1)

            dve.wait_ge(pads_ready, 1)
            dve.tensor_reduce(end_lane[:], ends[:], AX_X, ALU.max).then_inc(lanes_ready, 1)
            dve.wait_ge(lanes_ready, 1)
            dve.tensor_scalar(dsk[:, :, 0], best[:, :, 0], end_lane[:, 0:1], None, ALU.mult).then_inc(lanes_ready, 1)
            dve.tensor_scalar(cost[:, 0, 0:1], end_lane[:, 0:1], -BIG, BIG, ALU.mult, ALU.add
                              ).then_inc(lanes_ready, 1)
            dve.wait_ge(lanes_ready, 3)
            to_right = [min(lane + 1, 31) for lane in range(32)]
            to_left = [max(lane - 1, 0) for lane in range(32)]
            went_left, went_up, went_diag = mask_views(0, STEPS)
            dve.wait_ge(marks_ready, 1)
            for s in range(STEPS):
                if s:
                    dve.wait_ge(cost_ready, s)
                dve.stream_shuffle(edge[:, s % 2:s % 2 + 1], cost[:, s, W:W + 1], to_right).then_inc(inputs_ready, 1)
                dve.tensor_tensor(best[:, s, 1:W + 1], cost[:, s, 0:W], cost[:, s, 1:W + 1], ALU.min
                                  ).then_inc(inputs_ready, 1)
                if s:
                    dve.tensor_tensor(went_left[:, s - 1], cost[:, s, 0:W], best[:, s - 1, 1:W + 1], ALU.is_lt
                                      ).then_inc(compared, 1)
                if s in DIST_BOUNDS:
                    dve.wait_ge(dsk_in[DIST_BOUNDS.index(s)], 16)
                dve.wait_ge(inputs_ready, 2 * (s + 1))
                dve.tensor_tensor_scan(cost[:, s + 1, :], best[:, s, :], dsk[:, s, :], edge[:, s % 2:s % 2 + 1],
                                       ALU.min, ALU.add).then_inc(cost_ready, 1)
                dve.tensor_tensor(is_up[:, s], cost[:, s, 0:W], cost[:, s, 1:W + 1], ALU.is_gt)
            dve.wait_ge(cost_ready, STEPS)
            dve.tensor_tensor(went_left[:, STEPS - 1], cost[:, STEPS, 0:W], best[:, STEPS - 1, 1:W + 1], ALU.is_lt
                              ).then_inc(compared, 1)
            dve.tensor_scalar(goes_on[:, :, 0], best[:, :, 0], 0.0, end_lane[:, 1:2], ALU.mult, ALU.is_equal)
            dve.tensor_copy(inflow[:, 2:3], end_lane[:, 1:2]).then_inc(back_inputs_ready, 1)
            last = slice(MASK_BOUNDS[-1], STEPS)
            dve.wait_ge(compared, STEPS)
            dve.tensor_tensor(went_up[:, last], is_up[:, last], went_left[:, last], ALU.is_gt)
            dve.scalar_tensor_tensor(went_diag[:, last], went_left[:, last], -1.0, is_up[:, last], ALU.mult,
                                     ALU.is_equal).then_inc(last_mask, 1)
            dve.wait_ge(mask_ready, 3 * (len(MASK_BOUNDS) - 1))
            dve.wait_ge(last_mask, 1)
            for mask in (goes_on, leaves):
                dve.stream_shuffle(mask[:, 0:STEPS - 1, 1], mask[:, 1:STEPS, 2 * W + 1], to_left
                                   ).then_inc(marks_ready, 1)
            dve.wait_ge(marks_ready, 4)
            for n, s in enumerate(reversed(range(STEPS))):
                if n:
                    dve.wait_ge(path_ready, n)
                dve.stream_shuffle(edge[:, s % 2:s % 2 + 1], path[:, s + 1, 2 * W:2 * W + 1], to_left
                                   ).then_inc(back_inputs_ready, 1)
                if n:
                    dve.tensor_tensor(inflow[:].rearrange("l (k t) -> l k t", t=2),
                                      path[:, s + 1, 0::2].unsqueeze(2).to_broadcast([LANES, W + 1, 2]),
                                      leaves[:, s + 1, :].rearrange("l (k t) -> l k t", t=2), ALU.mult
                                      ).then_inc(back_inputs_ready, 1)
                dve.wait_ge(back_inputs_ready, 2 * (n + 1))
                dve.tensor_tensor_scan(path[:, s, 0:PAIRS - 1], goes_on[:, s, 0:PAIRS - 1], inflow[:, 0:PAIRS - 1],
                                       edge[:, s % 2:s % 2 + 1], ALU.mult, ALU.max).then_inc(path_ready, 1)

            for b in range(B + 1):
                if b < B:
                    t = batch_tiles(b)
                    dve.wait_ge(added_in_psum, b + 1)
                    dve.tensor_tensor(x2[:, t, :].rearrange("p n d -> p (n d)"), banks[b][:],
                                      x_sb[:, t, :].rearrange("p n d -> p (n d)"), ALU.add).then_inc(x2_ready, 1)
                    dve.wait_ge(x2_ready, b + 1)
                    norm_stats(x2, b, stats2_ready, var2_ready)
                if b:
                    t = batch_tiles(b - 1)
                    dve.wait_ge(sd2_ready, b)
                    dve.reciprocal(rstd[:, t], sd[:, t]).then_inc(rstd2_ready, 1)
                    dve.wait_ge(rstd2_ready, b)
                    dve.scalar_tensor_tensor(shift[:, t], mv[:, t, 0], -1.0, rstd[:, t], ALU.mult, ALU.mult
                                             ).then_inc(shift_ready, 1)
            for b in range(B):
                dve.wait_ge(y2T_hi_ready, b + 1)
                dve.tensor_tensor(yT_lo[:, b * S:(b + 1) * S], banks[4 + b][:], yT_hi[:, b * S:(b + 1) * S],
                                  ALU.subtract).then_inc(y2T_lo_ready, 1)

            def per_tile(v):
                return v.unsqueeze(2).to_broadcast([P, TILES, E])

            def per_expert(v):
                return v.unsqueeze(1).to_broadcast([P, TILES, E])

            def each_tile(v, n=TILES):
                return v.unsqueeze(2).to_broadcast([P, E, n])

            steps = [0]

            def routed(ins):
                steps[0] += 1
                ins.then_inc(route, 1)
                dve.wait_ge(route, steps[0])

            dve.wait_ge(logits_in_psum, 1)
            dve.scalar_tensor_tensor(logits[:], banks[0][:, 0:TILES * E].rearrange("p (n e) -> p n e", e=E),
                                     1.0 / WSCALE, per_expert(gate_b_sb[:]), ALU.mult, ALU.add).then_inc(logits_ready, 1)
            dve.wait_ge(score_ready, 1)
            for k, sc in enumerate((score, score2)):
                routed(dve.tensor_reduce(top[:, k, :], sc[:], AX_X, ALU.max))
                routed(dve.tensor_tensor(is_top[:], sc[:], per_tile(top[:, k, :]), ALU.is_equal))
                routed(dve.tensor_tensor(key[:], is_top[:], per_expert(rank_key[:]), ALU.mult))
                routed(dve.tensor_reduce(key_top[:], key[:], AX_X, ALU.max))
                routed(dve.tensor_tensor(pick[:, k], key[:], per_tile(key_top[:]), ALU.is_equal))
                if k == 0:
                    routed(dve.scalar_tensor_tensor(score2[:], pick[:, 0], -4.0, score[:], ALU.mult, ALU.add))
            dve.tensor_tensor(picked[:], pick[:, 0], pick[:, 1], ALU.add).then_inc(picked_ready, 1)
            routed(dve.scalar_tensor_tensor(denom[:], top[:, 0, :], 1e-6, top[:, 1, :], ALU.add, ALU.add))
            routed(dve.reciprocal(denom[:], denom[:]))
            for k in range(TOP):
                routed(dve.tensor_tensor(weight[k], top[:, k, :], denom[:], ALU.mult))
            dve.wait_ge(ranks_in_psum, 1)
            routed(dve.tensor_copy(in_tile[:], banks[5][:, 0:P].rearrange("p (n e) -> p e n", e=E)))
            routed(dve.tensor_tensor_scan(running[:].rearrange("p e n -> p (e n)"),
                                          carry_on[:].rearrange("p e n -> p (e n)"),
                                          in_tile[:].rearrange("p e n -> p (e n)"), 0.0, ALU.mult, ALU.add))
            routed(dve.tensor_tensor(exceeds[:], each_tile(running[:, :, TILES - 1], TILES_EACH),
                                     thresholds[:].unsqueeze(1).to_broadcast([P, E, TILES_EACH]), ALU.is_gt))
            routed(dve.tensor_tensor(offset[:], running[:], in_tile[:], ALU.subtract))
            routed(dve.tensor_reduce(tiles_of[:], exceeds[:], AX_X, ALU.add))
            routed(dve.tensor_tensor_scan(tiles_upto[:], ones[:, 0:E], tiles_of[:], 0.0, ALU.mult, ALU.add))
            routed(dve.tensor_tensor(tiles_before[:], tiles_upto[:], tiles_of[:], ALU.subtract))
            routed(dve.scalar_tensor_tensor(offset[:], each_tile(tiles_before[:]), float(ET), offset[:], ALU.mult, ALU.add))
            routed(dve.tensor_tensor(place[:], banks[4][:, 0:P].rearrange("p (n e) -> p n e", e=E),
                                     offset[:].rearrange("p e n -> p n e"), ALU.add))
            for k in range(TOP):
                routed(dve.tensor_tensor(part[:, k], pick[:, k], place[:], ALU.mult))
            routed(dve.tensor_reduce(slot_f[:], part[:], AX_X, ALU.add))
            dve.tensor_copy(slot[:], slot_f[:].rearrange("p k n -> p (k n)")).then_inc(slots_ready, 1)
            for k in range(TOP):
                routed(dve.scalar_tensor_tensor(part[:, k], pick[:, k], WSCALE, per_tile(weight[k]),
                                                ALU.mult, ALU.mult))
            dve.tensor_tensor(gates[:, :, 0:E], part[:, 0], part[:, 1], ALU.add).then_inc(gates_ready, 1)
            def every_tile(v):
                return v.unsqueeze(1).to_broadcast([P, EXPERT_TILES, E])

            tile_nos = tile_no[:].unsqueeze(2).to_broadcast([P, EXPERT_TILES, E])
            routed(dve.tensor_tensor(past[:], every_tile(tiles_upto[:]), tile_nos, ALU.is_le))
            routed(dve.tensor_reduce(tile_expert_f[:], past[0:1], AX_X, ALU.add))
            dve.tensor_scalar(tile_expert[:], tile_expert_f[:], float(E - 1), None, ALU.min).then_inc(table_ready, 1)
            def shared():
                def keep_sum(b):
                    dve.wait_ge(s_down_done, b + 1)
                    dve.tensor_copy(acc[:, b * S:(b + 1) * S], banks[S_DOWN_BANKS[b % 2]][:]).then_inc(acc_ready, 1)

                for n in range(B * NCH):
                    b, c = n // NCH, n % NCH
                    if c == 0 and b >= S_SLOTS:
                        keep_sum(b - S_SLOTS)
                    dve.wait_ge(s_gelu_done, n + 1)
                    dve.tensor_copy(shared_hi[:, b % S_SLOTS, c, :], shared_g[:, n % 2, :]).then_inc(s_hi_ready, 1)
                    dve.wait_ge(s_hi_ready, n + 1)
                    dve.tensor_tensor(shared_lo[:, b % S_SLOTS, c, :], shared_g[:, n % 2, :],
                                      shared_hi[:, b % S_SLOTS, c, :], ALU.subtract).then_inc(s_hid_ready, 1)

                for b in range(B - S_SLOTS, B):
                    keep_sum(b)

            def x_low(j, k):
                dve.wait_ge(xT_hi_ready, j + 1)
                dve.tensor_tensor(xT_lo[:, k, :], banks[XT_BANKS[k]][:, 0:ET], xT_hi[:, k, :], ALU.subtract
                                  ).then_inc(xT_ready, 1)

            def hidden_halves(j, k, first=False):
                for m in range(HALVES):
                    dve.wait_ge(gelu_done, j * HALVES + (m + 1))
                    if m == 0 and not first:
                        dve.wait_ge(y_done, j - 1)
                    dve.tensor_copy(hid_hi[:, k, m, :], hid[:, k, m, :]).then_inc(hid_hi_ready, 1)
                    dve.wait_ge(hid_hi_ready, j * HALVES + (m + 1))
                    dve.tensor_tensor(hid_lo[:, k, m, :], hid[:, k, m, :], hid_hi[:, k, m, :], ALU.subtract
                                      ).then_inc(hid_ready, 1)

            shared()
            routed(dve.tensor_tensor(started[:], every_tile(tiles_before[:]), tile_nos, ALU.is_le))
            routed(dve.tensor_tensor(started[:], started[:], past[:], ALU.subtract))
            dve.wait_ge(up_bias_ready, 1)
            for c in range(NCH):
                routed(dve.tensor_tensor(past[:], started[:], every_tile(up_bias[:, 0:E, c]), ALU.mult))
                ins = dve.tensor_reduce(tile_bias[:, :, c], past[:], AX_X, ALU.add)
                ins.then_inc(tile_bias_ready, 1)
                dve.wait_ge(tile_bias_ready, c + 1)
            for k in range(SLOTS):
                x_low(k, k)
            for k in range(SLOTS):
                hidden_halves(k, k, first=True)
                x_low(SLOTS + k, k)
            with dve.Fori(1, ROUNDS - 1) as i:
                for k in range(SLOTS):
                    hidden_halves(i * SLOTS + k, k)
                    x_low(i * SLOTS + (k + SLOTS), k)
            for k in range(SLOTS):
                hidden_halves(EXPERT_TILES - SLOTS + k, k)

            for b in range(B):
                tot = total[:, b % 2]
                flat = tot.rearrange("p n d -> p (n d)")
                dve.wait_ge(pair_ready, b + 1)
                dve.tensor_tensor(flat, by_token[0][:, b * S:(b + 1) * S], acc[:, b * S:(b + 1) * S], ALU.add
                                  ).then_inc(tail, 1)
                dve.wait_ge(tail, 5 * b + 1)
                dve.tensor_reduce(peak[:, b, :], tot, AX_X, ALU.max, apply_absolute_value=True).then_inc(tail, 1)
                dve.wait_ge(tail, 5 * b + 2)
                dve.tensor_scalar(peak_eps[:, b, :], peak[:, b, :], OUT_SCALE / WSCALE, 1e-6, ALU.mult, ALU.add
                                  ).then_inc(tail, 1)
                dve.wait_ge(tail, 5 * b + 3)
                dve.reciprocal(peak[:, b, :], peak_eps[:, b, :]).then_inc(tail, 1)
                dve.wait_ge(tail, 5 * b + 4)
                dve.tensor_scalar(inv_peak[:, b, :], peak[:, b, :], OUT_SCALE / WSCALE, None, ALU.mult
                                  ).then_inc(tail, 1)
                dve.wait_ge(tail, 5 * b + 5)
                if b >= 2:
                    dve.wait_ge(out_done[b % 2], 16 * (b // 2))
                for n in range(TPB):
                    ins = dve.scalar_tensor_tensor(result[:, b % 2, n, :], tot[:, n, :], inv_peak[:, b, n:n + 1],
                                                   x2[:, b * TPB + n, :], ALU.mult, ALU.add)
                ins.then_inc(result_ready, 1)


_INS = ["x", "ctx_1024"] + ["L0_ffn_" + n for n in ("gate_w", "bias", "up_w", "up_b", "down_w", "down_b",
                                                   "sw_up", "sb_up", "sw_down", "sb_down")]


def kernel(**inputs):
    import numpy as np
    import concourse.bacc as bacc
    from concourse.bass_utils import run_bass_kernel_spmd

    nc = bacc.Bacc("TRN2", target_bir_lowering=False, num_devices=1)
    arrays, args = {}, []
    for name in _INS:
        a = np.ascontiguousarray(inputs[name])
        arrays[f"in_{name}"] = a
        args.append(nc.dram_tensor(f"in_{name}", a.shape, mybir.dt.from_np(a.dtype), kind="ExternalInput").ap())
    args.append(nc.dram_tensor("out_0", (B, S, H), F32, kind="ExternalOutput").ap())
    build(nc, *args)
    r = run_bass_kernel_spmd(nc, [arrays], core_ids=[0])
    return r.results[0]["out_0"]
```

```python
from contextlib import ExitStack

import concourse.bass as bass
from concourse import mybir

F32 = mybir.dt.float32
F16 = mybir.dt.float16
U32 = mybir.dt.uint32
ALU = mybir.AluOpType
ACT = mybir.ActivationFunctionType
AX_X = mybir.AxisListType.X

P = 128
B, S, H = 4, 512, 128
SMALL = 77
TILES = B * S // P
TPB = S // P
BLOCKS = 16
W = S // BLOCKS
STEPS = SMALL + BLOCKS - 1
LANES = B * BLOCKS
DIST_BOUNDS = 0, 4, 16, 40, STEPS
MASK_BOUNDS = 0, 24, 48, 66, 80, 88
MASK_STEPS = max(b - a for a, b in zip(MASK_BOUNDS, MASK_BOUNDS[1:]))
BPT = BLOCKS // TPB
PATH_BOUNDS = STEPS, 64, 40, 16, *range(BPT * (TPB - 1), -1, -BPT)
PAIRS = 2 * (W + 1)
POOL_TILES = 0, 2, 2, 1
DVE_TILES = 1, 2, 2, 3
PAD = BLOCKS - 1
PITCH = B * S
DRAM_ROWS = SMALL + 2 * PAD + (B - 1) * BLOCKS
BIG = 1e30
EPS = 1e-5
E, TOP = 8, 2
I = 4 * H
NCH = I // P
SLOTS = 2
S_SLOTS = 3
S_LAG = NCH + 2
UNROLL = 4
HALVES = 2
ET = 2 * P
PARTS = ET // P
TILES_EACH = B * S // ET
EXPERT_TILES = (TOP * B * S + E * (ET - 1)) // ET
LOADED_TILES = -(-EXPERT_TILES // SLOTS) * SLOTS
ROUNDS = LOADED_TILES // SLOTS
WSCALE = 256.0
OUT_SCALE = 0.1


def build(nc, x, ctx_in, gate_w, gate_b, up_w, up_b, down_w, down_b, sw_up, sb_up, sw_down, sb_down, out):
    with ExitStack() as stack:
        def sb(name, shape, dt=F32):
            return stack.enter_context(nc.sbuf_tensor(name, shape, dt))

        def sem(name):
            return stack.enter_context(nc.semaphore(name))

        banks = [stack.enter_context(nc.psum_tensor(f"bank{i}", [P, 512], F32)) for i in range(8)]

        arena_a = sb("arena_a", [P, STEPS * (W + 1)])
        arena_b = sb("arena_b", [P, max((STEPS + 1) * (W + 1), S_SLOTS * NCH * S // 2)])
        arena_c = sb("arena_c", [P, STEPS * (W + 1)])
        arena_d = sb("arena_d", [P, STEPS * PAIRS])
        dsk = arena_a[0:LANES, :].rearrange("l (s w) -> l s w", w=W + 1)
        cost = arena_b[0:LANES, 0:(STEPS + 1) * (W + 1)].rearrange(
            "l (s w) -> l s w", w=W + 1)
        best = arena_c[0:LANES, :].rearrange("l (s w) -> l s w", w=W + 1)
        arena_f = sb("arena_f", [P, STEPS * PAIRS])
        arena_g = sb("arena_g", [P, (STEPS + 1) * PAIRS])
        goes_on = arena_d[0:LANES, :].rearrange("l (s c) -> l s c", c=PAIRS)
        leaves = arena_f[0:LANES, :].rearrange("l (s c) -> l s c", c=PAIRS)
        path = arena_g[0:LANES, :].rearrange("l (s c) -> l s c", c=PAIRS)
        path_cells = arena_b[0:LANES, 0:STEPS * W].rearrange("l (s w) -> l s w", w=W)
        inflow = sb("inflow", [LANES, PAIRS])
        edge = sb("edge", [LANES, 2])
        ends = sb("ends", [LANES, 2, B])
        end_lane = sb("end_lane", [LANES, 2])
        big = sb("big", [PAD, S])

        x_sb = sb("x_sb", [P, TILES, H])
        ctx_sb = sb("ctx_sb", [SMALL, B, H])
        ident = sb("ident", [P, P])
        ones = sb("ones", [P, SMALL])
        eps = sb("eps", [P, 1])
        stats = sb("stats", [P, TILES, 6])
        mv = sb("mv", [P, TILES, 2])
        sd = sb("sd", [P, TILES])
        rstd = sb("rstd", [P, TILES])
        shift = sb("shift", [P, TILES])
        row_and_place = sb("row_and_place", [P, TILES, H + 2])
        y = row_and_place[:, :, 0:H]
        yT = arena_f[:, 0:B * S].rearrange("p (b s) -> p b s", s=S)
        ysqT = arena_f[:, B * S:2 * B * S].rearrange("p (b s) -> p b s", s=S)
        ctxm2T = sb("ctxm2T", [P, B, SMALL])
        ctxsq = sb("ctxsq", [SMALL, H])
        aa = sb("aa", [SMALL, B])
        dist = sb("dist", [SMALL, B, S])
        path_rows = dist
        x2 = sb("x2", [P, TILES, H])
        is_up = arena_g[0:LANES, 0:STEPS * W].rearrange("l (s w) -> l s w", w=W)
        stays = x2[0:LANES].rearrange("p n d -> p (n d)")[:, 0:MASK_STEPS * W].rearrange("l (s w) -> l s w", w=W)

        stage = sb("stage", [P, 2, I])
        up_hi = sb("up_hi", [P, (E + 1) * I], F16)
        up_lo = sb("up_lo", [P, (E + 1) * I], F16)
        down_hi = sb("down_hi", [P, (E + 1) * I], F16)
        down_lo = sb("down_lo", [P, (E + 1) * I], F16)
        gate_ld = sb("gate_ld", [P, E])
        gate_hi = sb("gate_hi", [P, E], F16)
        gate_lo = sb("gate_lo", [P, E], F16)
        gate_b_sb = sb("gate_b_sb", [P, E])
        bias_ld = sb("bias_ld", [(E + 1) * NCH, P])
        up_bias = sb("up_bias", [P, E + 1, NCH])
        tile_bias = sb("tile_bias", [P, EXPERT_TILES, NCH])
        down_b_all = sb("down_b_all", [E + 1, H])

        same_token = sb("same_token", [P, TILES, E])
        logits = sb("logits", [P, TILES, E])
        score = sb("score", [P, TILES, E])
        score2 = sb("score2", [P, TILES, E])
        top = sb("top", [P, TOP, TILES])
        is_top = sb("is_top", [P, TILES, E])
        met = sb("met", [P, TILES, E])
        pick = sb("pick", [P, TOP, TILES, E])
        picked = sb("picked", [P, TILES, E], F16)
        denom = sb("denom", [P, TILES])
        part = sb("part", [P, TOP, TILES, E])
        gates = sb("gates", [P, TILES, E + 1])
        not_earlier = sb("not_earlier", [P, P], F16)
        ones16 = sb("ones16", [P, P], F16)
        carry_on = sb("carry_on", [P, E, TILES])
        thresholds = sb("thresholds", [P, TILES_EACH])
        tile_no = sb("tile_no", [P, EXPERT_TILES])
        running = sb("running", [P, E, TILES])
        offset = sb("offset", [P, E, TILES])
        exceeds = sb("exceeds", [P, E, TILES_EACH])
        tiles_of = sb("tiles_of", [P, E])
        tiles_upto = sb("tiles_upto", [P, E])
        tiles_before = sb("tiles_before", [P, E])
        place = sb("place", [P, TILES, E])
        slot = sb("slot", [P, TOP * TILES], U32)
        past = sb("past", [P, EXPERT_TILES, E])
        started = sb("started", [P, EXPERT_TILES, E])
        tile_expert_f = sb("tile_expert_f", [1, EXPERT_TILES])
        tile_expert = sb("tile_expert", [1, EXPERT_TILES], U32)

        yT_hi = arena_a[:, 0:TILES * P // 2].bitcast(F16)
        yT_lo = arena_a[:, TILES * P // 2:TILES * P].bitcast(F16)
        by_token = arena_b[:, 0:TILES * H], arena_c[:, 0:TILES * H]
        acc = arena_d[:, 0:TILES * H]
        gatesT = ysqT[0:E + 1, :, :].rearrange("e b s -> e (b s)")

        def within(arena, start, shape, dt=F32):
            n = 1
            for m in shape:
                n *= m
            n = n // 2 if dt == F16 else n
            view = arena[:, start:start + n]
            view = view.bitcast(F16) if dt == F16 else view
            names = " ".join("abc"[:len(shape)])
            sizes = dict(zip("abc", shape))
            return view.rearrange(f"p ({names}) -> p {names}", **sizes), start + n

        x_flat = x_sb[:].rearrange("p n d -> p (n d)")
        total, at = within(x_flat, 0, (2, TPB, H))
        result, at = within(x_flat, at, (2, TPB, H))
        hid, at = within(arena_f, 0, (SLOTS, HALVES, I * PARTS // HALVES))
        hid_hi, at = within(arena_d, TILES * H, (SLOTS, HALVES, I * PARTS // HALVES), F16)
        shared_hi, _ = within(arena_b, 0, (S_SLOTS, NCH, S), F16)
        y_row, at = within(arena_d, at, (SLOTS, PARTS, H))
        xT_hi, at = within(arena_d, at, (SLOTS, ET), F16)
        xT_lo, at = within(arena_a, TILES * P, (SLOTS, ET), F16)
        hid_lo, at = within(arena_g, 0, (SLOTS, HALVES, I * PARTS // HALVES), F16)
        shared_g, at = within(arena_g, at, (2, S))
        shared_lo, at = within(arena_g, at, (S_SLOTS, NCH, S), F16)
        x_row, at = within(arena_g, at, (SLOTS, PARTS, H + 2))
        row_and_place2, at = within(arena_c, 0, (TILES, H + 2))
        weight = row_and_place[:, :, H + 1], row_and_place2[:, :, H + 1]
        padding = sb("padding", [P, H + 2])
        result_weight = sb("result_weight", [P, EXPERT_TILES * PARTS])
        result_place = sb("result_place", [P, EXPERT_TILES * PARTS], U32)
        peak = sb("peak", [P, B, TPB])
        peak_eps = sb("peak_eps", [P, B, TPB])
        inv_peak = sb("inv_peak", [P, B, TPB])

        dist_dram = nc.dram_tensor("dist_dram", (DRAM_ROWS, PITCH), F32, kind="Internal")
        path_dram = nc.dram_tensor("path_dram", (DRAM_ROWS, PITCH), F32, kind="Internal")
        sorted_dram = nc.dram_tensor("sorted_dram", (LOADED_TILES * ET, H + 2), F32, kind="Internal")
        expert_dram = nc.dram_tensor("expert_dram", (TOP * B * S, H), F32, kind="Internal")

        x_in = [sem(f"x_in{b}") for b in range(B)]
        ctx_ld = sem("ctx_ld")
        small_ld = sem("small_ld")
        stage_ld = [sem(f"stage_ld{i}") for i in range(2)]
        const_ready = sem("const_ready")
        pads_ready = sem("pads_ready")
        big_ready = sem("big_ready")
        ffn_const_ready = sem("ffn_const_ready")
        pool_step = sem("pool_step")
        stats_ready = sem("stats_ready")
        var_ready = sem("var_ready")
        sd_ready = sem("sd_ready")
        rstd_ready = sem("rstd_ready")
        y_ready = sem("y_ready")
        yT_in_psum = sem("yT_in_psum")
        yT_ready = sem("yT_ready")
        ctxT_in_psum = sem("ctxT_in_psum")
        ctxT_ready = sem("ctxT_ready")
        aa_ready = sem("aa_ready")
        d2_in_psum = sem("d2_in_psum")
        d2_ready = sem("d2_ready")
        dist_ready = sem("dist_ready")
        pad_out = sem("pad_out")
        dist_out = sem("dist_out")
        dsk_in = [sem(f"dsk_in{k}") for k in range(len(DIST_BOUNDS) - 1)]
        lanes_ready = sem("lanes_ready")
        inputs_ready = sem("inputs_ready")
        back_inputs_ready = sem("back_inputs_ready")
        cost_ready = sem("cost_ready")
        mask_ready = sem("mask_ready")
        cells_ready = sem("cells_ready")
        marks_ready = sem("marks_ready")
        last_mask = sem("last_mask")
        compared = sem("compared")
        path_ready = sem("path_ready")
        path_out = [sem(f"path_out{k}") for k in range(len(PATH_BOUNDS) - 1)]
        rows_in = [sem(f"rows_in{g}") for g in range(TPB)]
        added_in_psum = sem("added_in_psum")
        x2_ready = sem("x2_ready")
        scaled_ready = sem("scaled_ready")
        halves_hi = sem("halves_hi")
        halves_lo = sem("halves_lo")
        small_hi = sem("small_hi")
        biasT_in_psum = sem("biasT_in_psum")
        up_bias_ready = sem("up_bias_ready")
        tile_bias_ready = sem("tile_bias_ready")
        weights_ready = sem("weights_ready")
        stats2_ready = sem("stats2_ready")
        var2_ready = sem("var2_ready")
        sd2_ready = sem("sd2_ready")
        rstd2_ready = sem("rstd2_ready")
        shift_ready = sem("shift_ready")
        y2_by_dve = sem("y2_by_dve")
        y2_ready = sem("y2_ready")
        y2T_in_psum = sem("y2T_in_psum")
        y2T_hi_ready = sem("y2T_hi_ready")
        y2T_lo_ready = sem("y2T_lo_ready")
        logits_in_psum = sem("logits_in_psum")
        logits_ready = sem("logits_ready")
        score_ready = sem("score_ready")
        route = sem("route")
        aside_ready = sem("aside_ready")
        picked_ready = sem("picked_ready")
        ranks_in_psum = sem("ranks_in_psum")
        gates_ready = sem("gates_ready")
        gatesT_in_psum = sem("gatesT_in_psum")
        gatesT_ready = sem("gatesT_ready")
        slots_ready = sem("slots_ready")
        table_ready = sem("table_ready")
        zeroed = sem("zeroed")
        scattered = sem("scattered")
        second_rows = sem("second_rows")
        place_kept = sem("place_kept")
        x_row_in = [sem(f"x_row_in{k}") for k in range(SLOTS)]
        xT_in_psum = sem("xT_in_psum")
        xT_hi_ready = sem("xT_hi_ready")
        xT_ready = sem("xT_ready")
        up_done = sem("up_done")
        gelu_done = sem("gelu_done")
        hid_hi_ready = sem("hid_hi_ready")
        hid_ready = sem("hid_ready")
        y_done = sem("y_done")
        y_row_ready = sem("y_row_ready")
        y_row_out = [sem(f"y_row_out{k}") for k in range(SLOTS)]
        s_up_done = sem("s_up_done")
        s_gelu_done = sem("s_gelu_done")
        s_hi_ready = sem("s_hi_ready")
        s_hid_ready = sem("s_hid_ready")
        s_down_done = sem("s_down_done")
        acc_ready = sem("acc_ready")
        by_token_in = [sem(f"by_token_in{b}") for b in range(B)]
        pair_ready = sem("pair_ready")
        tail = sem("tail")
        total_ready = sem("total_ready")
        peak_ready = sem("peak_ready")
        result_ready = sem("result_ready")
        scaled_by_act = sem("scaled_by_act")
        result_by_pool = sem("result_by_pool")
        out_done = [sem(f"out_done{i}") for i in range(2)]

        x_tiles = x.rearrange("b (n p) d -> b p n d", p=P)
        out_tiles = out.rearrange("b (n p) d -> b p n d", p=P)
        UP_BANK = 0
        XT_BANKS = 4, 7
        S_DOWN_BANKS = 7, 5
        S_UP_BANKS = 6, 3
        Y_BANKS = 5, 6

        def batch_tiles(b):
            return slice(b * TPB, (b + 1) * TPB)

        def group_tiles(g):
            return slice(TPB - 1 - g, TILES, TPB)

        def group_list(g):
            return list(range(TPB - 1 - g, TILES, TPB))

        def skewed(dram, s0, s1):
            return bass.AP(tensor=dram, offset=(PAD + s0 - (BLOCKS - 1)) * PITCH + B * S - W,
                           ap=[[PITCH - W, LANES], [PITCH, s1 - s0], [1, W]])

        def matrix_rows(dram, r0, r1, b0=0, b1=B, c0=0, c1=S):
            return bass.AP(tensor=dram, offset=(PAD + r0 + BLOCKS * b0) * PITCH + (B - 1 - b0) * S + c0,
                           ap=[[PITCH, r1 - r0], [BLOCKS * PITCH - S, b1 - b0], [1, c1 - c0]])

        def tiles_of_yT(v, g):
            return v.rearrange("p (t c) -> p t c", c=P)[:, group_tiles(g), :]

        def mask_views(s0, s1):
            odd, even = slice(2 * W + 1, 1, -2), slice(2 * W, 0, -2)
            return goes_on[:, s0:s1, odd], leaves[:, s0:s1, even], leaves[:, s0:s1, odd]

        block = stack.enter_context(nc.Block())

        @block.sync
        def _(sp):
            for b in range(B):
                sp.dma_start(x_sb[:, batch_tiles(b), :], x_tiles[b]).then_inc(x_in[b], 16)
            sp.wait_ge(big_ready, 1)
            for r0 in (-PAD, SMALL):
                sp.dma_start(matrix_rows(dist_dram, r0, r0 + PAD), big[:].unsqueeze(1).to_broadcast([PAD, B, S])
                             ).then_inc(pad_out, 16)
            for b in range(B):
                sp.wait_ge(dist_ready, b + 1)
                sp.dma_start(matrix_rows(dist_dram, 0, SMALL, b, b + 1), dist[:, b:b + 1, :]).then_inc(dist_out, 16)
            sp.wait_ge(pad_out, 16 * 2)
            sp.wait_ge(dist_out, 16 * B)
            for k, (s0, s1) in enumerate(zip(DIST_BOUNDS, DIST_BOUNDS[1:])):
                sp.dma_start(dsk[:, s0:s1, 1:W + 1], skewed(dist_dram, s0, s1)).then_inc(dsk_in[k], 16)
            sp.dma_start(bias_ld[0:E * NCH, :], up_b.rearrange("e (c p) -> (e c) p", p=P)).then_inc(small_ld, 16)
            sp.dma_start(bias_ld[E * NCH:(E + 1) * NCH, :], sb_up.rearrange("(c p) -> c p", p=P)
                         ).then_inc(small_ld, 16)
            sp.dma_start(gate_ld[:], gate_w).then_inc(small_ld, 16)
            sp.dma_start(gate_b_sb[:], gate_b.partition_broadcast(P)).then_inc(small_ld, 16)
            sp.dma_start(down_b_all[0:E, :], down_b).then_inc(small_ld, 16)
            sp.dma_start(down_b_all[E:E + 1, :], sb_down.rearrange("(a d) -> a d", a=1)).then_inc(small_ld, 16)
            sp.wait_ge(ffn_const_ready, 1)
            pads = sorted_dram.ap().rearrange("(j p) d -> p j d", p=P)
            sp.dma_start(pads, padding[:].unsqueeze(1).to_broadcast([P, LOADED_TILES * PARTS, H + 2])
                         ).then_inc(zeroed, 16)
            for e in range(E + 1):
                for m in range(2):
                    n = 2 * e + m
                    if n >= 2:
                        sp.wait_ge(halves_lo, n - 1)
                    if m == 0:
                        sp.dma_start(stage[:, 0, :], up_w[e] if e < E else sw_up).then_inc(stage_ld[0], 16)
                    else:
                        src = down_w[e] if e < E else sw_down
                        sp.dma_start(stage[:, 1, :].rearrange("p (c d) -> p c d", d=H),
                                     src.rearrange("(c p) d -> p c d", p=P)).then_inc(stage_ld[1], 16)
            for k, (s1, s0) in enumerate(zip(PATH_BOUNDS, PATH_BOUNDS[1:])):
                if s0 % BPT == 0 and s0 // BPT < TPB:
                    n = s0 // BPT
                    for piece in path_out[0 if n == TPB - 1 else k:k + 1]:
                        sp.wait_ge(piece, 16)
                    cols = slice(n * P, (n + 1) * P)
                    sp.dma_start(path_rows[:, :, cols], matrix_rows(path_dram, 0, SMALL, c0=cols.start, c1=cols.stop)
                                 ).then_inc(rows_in[TPB - 1 - n], 16)

            def load(j, k):
                rows = sorted_dram.ap()[bass.ds(j * ET, ET), :].rearrange("(n p) d -> p n d", p=P)
                sp.dma_start(x_row[:, k], rows).then_inc(x_row_in[k], 16)

            sp.wait_ge(scattered, 16 * TOP * TILES)
            for k in range(SLOTS):
                load(k, k)
            with sp.Fori(0, ROUNDS - 1) as i:
                for k in range(SLOTS):
                    sp.wait_ge(xT_in_psum, i * SLOTS + (k + 1))
                    sp.wait_ge(place_kept, i * SLOTS + (k + 1))
                    load(i * SLOTS + (k + SLOTS), k)
            for k in range(SLOTS):
                sp.wait_ge(y_row_out[k], 16 * PARTS * len(range(k, EXPERT_TILES, SLOTS)))
            for b in range(B):
                for k in range(TOP):
                    first = k * B * S + b * S
                    sp.dma_start(by_token[k][:, b * S:(b + 1) * S].rearrange("p (n d) -> p n d", d=H),
                                 expert_dram.ap()[first:first + S, :].rearrange("(n p) d -> p n d", p=P)
                                 ).then_inc(by_token_in[b], 16)
            for b in range(B):
                sp.wait_ge(result_ready, b + 1)
                if sum(POOL_TILES[:b + 1]):
                    sp.wait_ge(result_by_pool, sum(POOL_TILES[:b + 1]))
                sp.dma_start(out_tiles[b], result[:, b % 2, :, :]).then_inc(out_done[b % 2], 16)
            for i in range(2):
                sp.wait_ge(out_done[i], 16 * B // 2)

        @block.gpsimd
        def _(pool):
            pool.memset(ident[:], 0.0).then_inc(pool_step, 1)
            pool.memset(ones[:], 1.0)
            pool.memset(eps[:], EPS)
            pool.wait_ge(pool_step, 1)
            pool.affine_select(out=ident[:], in_=ident[:], compare_op=ALU.not_equal, fill=1.0, base=0,
                               pattern=[[-1, P]], channel_multiplier=1).then_inc(const_ready, 1)
            pool.memset(big[:], BIG).then_inc(big_ready, 1)
            pool.memset(best[:, :, 0], BIG)
            pool.memset(cost[:, 0, :], BIG)
            pool.memset(ends[:], 0.0).then_inc(pool_step, 1)
            pool.wait_ge(pool_step, 2)
            for e in range(2):
                last = pool.affine_select(out=ends[:, e, :], in_=ends[:, e, :], compare_op=ALU.not_equal, fill=1.0,
                                          base=(e - 1) * (BLOCKS - 1), pattern=[[-BLOCKS, B]], channel_multiplier=1)
            last.then_inc(pads_ready, 1)
            pool.memset(goes_on[:, :, 2::2], 1.0)
            pool.memset(path[:, STEPS, :], 0.0)
            pool.memset(inflow[:], 0.0)
            pool.memset(goes_on[:, STEPS - 1, 1:2], 0.0).then_inc(marks_ready, 1)
            pool.memset(same_token[:], 1.0)
            pool.memset(gates[:, :, E], WSCALE)
            pool.memset(padding[:], 0.0)
            pool.memset(not_earlier[:], 0.0)
            pool.memset(ones16[:], 1.0)
            pool.memset(carry_on[:], 1.0)
            pool.iota(thresholds[:], pattern=[[ET, TILES_EACH]], base=0, channel_multiplier=0,
                      allow_small_or_imprecise_dtypes=True)
            pool.iota(row_and_place[:, :, H], pattern=[[P, TILES]], base=0, channel_multiplier=1,
                      allow_small_or_imprecise_dtypes=True)
            pool.iota(tile_no[:], pattern=[[1, EXPERT_TILES]], base=0, channel_multiplier=0,
                      allow_small_or_imprecise_dtypes=True).then_inc(pool_step, 1)
            pool.wait_ge(pool_step, 3)
            pool.memset(carry_on[:, :, 0], 0.0)
            pool.memset(same_token[:, :, 0], 0.0)
            pool.memset(padding[:, H:H + 1], float(TOP * B * S))
            pool.affine_select(out=not_earlier[:], in_=not_earlier[:], compare_op=ALU.is_ge, fill=-1.0, base=-1,
                               pattern=[[1, P]], channel_multiplier=-1).then_inc(ffn_const_ready, 1)
            pool.wait_ge(compared, 1)
            pool.memset(leaves[:, :, 0], 0.0)
            pool.memset(leaves[:, STEPS - 1, 1:2], 0.0).then_inc(marks_ready, 1)
            for k, (s0, s1) in enumerate(zip(MASK_BOUNDS, MASK_BOUNDS[1:])):
                went_left, went_up, went_diag = mask_views(s0, s1)
                not_left = stays[:, 0:s1 - s0, :]
                if k:
                    pool.wait_ge(mask_ready, 3 * k)
                pool.wait_ge(compared, s1)
                pool.tensor_scalar(not_left, went_left, -1.0, 1.0, ALU.mult, ALU.add).then_inc(mask_ready, 1)
                pool.wait_ge(mask_ready, 3 * k + 1)
                pool.tensor_tensor(went_up, is_up[:, s0:s1], not_left, ALU.mult).then_inc(mask_ready, 1)
                pool.wait_ge(mask_ready, 3 * k + 2)
                pool.tensor_tensor(went_diag, not_left, went_up, ALU.subtract).then_inc(mask_ready, 1)
            pool.wait_ge(small_hi, 1)
            pool.tensor_tensor(gate_lo[:], gate_ld[:], gate_hi[:], ALU.subtract).then_inc(weights_ready, 1)
            for e in range(E + 1):
                cols = slice(e * I, (e + 1) * I)
                for m, (hi, lo) in enumerate(((up_hi, up_lo), (down_hi, down_lo))):
                    pool.wait_ge(halves_hi, 2 * e + m + 1)
                    pool.tensor_tensor(lo[:, cols], stage[:, m, :], hi[:, cols], ALU.subtract).then_inc(halves_lo, 1)
            pool.wait_ge(marks_ready, 4)
            pool.iota(row_and_place2[:, :, H], pattern=[[P, TILES]], base=B * S, channel_multiplier=1,
                      allow_small_or_imprecise_dtypes=True).then_inc(second_rows, 1)
            for g in range(TPB):
                pool.wait_ge(y2_ready, g + 1)
                pool.wait_ge(y2_by_dve, sum(DVE_TILES[:g + 1]))
                pool.tensor_copy(row_and_place2[:, group_tiles(g), 0:H], y[:, group_tiles(g), :]
                                 ).then_inc(second_rows, 1)
            pool.wait_ge(zeroed, 16)
            for k, src in enumerate((row_and_place, row_and_place2)):
                pool.wait_ge(slots_ready, k + 1)
                if k:
                    pool.wait_ge(second_rows, 1 + B)
                for t in range(TILES):
                    pool.indirect_dma_start(
                        out=sorted_dram.ap(), in_=src[:, t, :], in_offset=None,
                        out_offset=bass.IndirectOffsetOnAxis(ap=slot[:, k * TILES + t:k * TILES + t + 1], axis=0)
                    ).then_inc(scattered, 16)

            def keep_place(j):
                pool.wait_ge(x_row_in[j % SLOTS], 16 * (j // SLOTS + 1))
                pool.tensor_copy(result_weight[:, j * PARTS:(j + 1) * PARTS], x_row[:, j % SLOTS, :, H + 1])
                pool.tensor_copy(result_place[:, j * PARTS:(j + 1) * PARTS], x_row[:, j % SLOTS, :, H]
                                 ).then_inc(place_kept, 1)

            ahead = 2 * SLOTS
            for j in range(ahead):
                keep_place(j)
            for j in range(EXPERT_TILES):
                if j + ahead < EXPERT_TILES:
                    keep_place(j + ahead)
                pool.wait_ge(place_kept, j + 1)
                pool.wait_ge(y_row_ready, j + 1)
                for n in range(PARTS):
                    place_of = result_place[:, j * PARTS + n:j * PARTS + n + 1]
                    pool.indirect_dma_start(
                        out=expert_dram.ap(), in_=y_row[:, j % SLOTS, n, :], in_offset=None,
                        out_offset=bass.IndirectOffsetOnAxis(ap=place_of, axis=0),
                        bounds_check=TOP * B * S - 1, oob_is_err=False
                    ).then_inc(y_row_out[j % SLOTS], 16)
            for b in range(B):
                cols = slice(b * S, (b + 1) * S)
                pool.wait_ge(by_token_in[b], 16 * TOP)
                pool.tensor_tensor(by_token[0][:, cols], by_token[0][:, cols], by_token[1][:, cols], ALU.add
                                   ).then_inc(pair_ready, 1)
            done = 0
            for b in range(B):
                for n in range(TPB - POOL_TILES[b], TPB):
                    done += 1
                    pool.wait_ge(scaled_by_act, done)
                    pool.tensor_tensor(result[:, b % 2, n, :], result[:, b % 2, n, :], x2[:, b * TPB + n, :], ALU.add
                                       ).then_inc(result_by_pool, 1)

        @block.scalar
        def _(act):
            act.dma_start(ctx_sb[:], ctx_in.rearrange("b i d -> i b d")).then_inc(ctx_ld, 16)
            act.wait_ge(ctx_ld, 16)
            for b in range(B):
                act.activation(ctxsq[:], ctx_sb[:, b, :], ACT.Square, accum_out=aa[:, b:b + 1]).then_inc(aa_ready, 1)
                act.wait_ge(aa_ready, b + 1)
            act.wait_ge(ctxT_in_psum, 1)
            act.mul(ctxm2T[:].rearrange("p b i -> p (b i)"), banks[7][:, 0:B * SMALL], -2.0).then_inc(ctxT_ready, 1)
            act.wait_ge(const_ready, 1)
            for b in range(B + 1):
                if b < B:
                    t = batch_tiles(b)
                    act.wait_ge(var_ready, b + 1)
                    act.activation(sd[:, t], mv[:, t, 1], ACT.Sqrt, bias=eps[:]).then_inc(sd_ready, 1)
                if b:
                    act.wait_ge(yT_in_psum, b)
                    act.activation(yT[:, b - 1, :], banks[b - 1][:], ACT.Copy).then_inc(yT_ready, 1)
                    act.activation(ysqT[:, b - 1, :], banks[b - 1][:], ACT.Square).then_inc(yT_ready, 1)
            for b in range(B):
                act.wait_ge(d2_ready, b + 1)
                act.activation(dist[:, b, :], dist[:, b, :], ACT.Sqrt).then_inc(dist_ready, 1)
            act.wait_ge(small_ld, 16 * 6)
            act.mul(gate_ld[:], gate_ld[:], WSCALE).then_inc(scaled_ready, 1)
            act.wait_ge(biasT_in_psum, 1)
            act.activation(up_bias[:].rearrange("p e c -> p (e c)"), banks[0][:, 0:(E + 1) * NCH], ACT.Copy
                           ).then_inc(up_bias_ready, 1)
            act.wait_ge(scaled_ready, 1)
            act.activation(gate_hi[:], gate_ld[:], ACT.Copy).then_inc(small_hi, 1)
            for e in range(E + 1):
                cols = slice(e * I, (e + 1) * I)
                for m, hi in enumerate((up_hi, down_hi)):
                    n = 2 * e + m
                    act.wait_ge(stage_ld[m], 16 * (e + 1))
                    act.mul(stage[:, m, :], stage[:, m, :], WSCALE).then_inc(scaled_ready, 1)
                    act.wait_ge(scaled_ready, n + 2)
                    act.activation(hi[:, cols], stage[:, m, :], ACT.Copy).then_inc(halves_hi, 1)
            for k, (s1, s0) in enumerate(zip(PATH_BOUNDS, PATH_BOUNDS[1:])):
                act.wait_ge(path_ready, STEPS - s0)
                act.activation(path_cells[:, s0:s1, :], path[:, s0:s1, 2 * W:0:-2], ACT.Copy).then_inc(cells_ready, 1)
                act.wait_ge(cells_ready, k + 1)
                act.dma_start(skewed(path_dram, s0, s1), path_cells[:, s0:s1, :]).then_inc(path_out[k], 16)
            for g in range(TPB + 2):
                if g < TPB:
                    t = group_tiles(g)
                    act.wait_ge(var2_ready, g + 1)
                    act.activation(sd[:, t], mv[:, t, 1], ACT.Sqrt, bias=eps[:]).then_inc(sd2_ready, 1)
                if 0 < g <= TPB:
                    act.wait_ge(shift_ready, g)
                    for t in group_list(g - 1)[:TPB - DVE_TILES[g - 1]]:
                        last = act.activation(y[:, t, :], x2[:, t, :], ACT.Identity, bias=shift[:, t:t + 1],
                                              scale=rstd[:, t:t + 1])
                    last.then_inc(y2_ready, 1)
                if g > 1:
                    act.wait_ge(y2T_in_psum, g - 1)
                    act.activation(tiles_of_yT(yT_hi, g - 2), banks[4 + g - 2][:].rearrange("p (b t) -> p b t", t=P),
                                   ACT.Copy).then_inc(y2T_hi_ready, 1)
            act.wait_ge(logits_ready, 1)
            act.activation(score[:], logits[:], ACT.Sigmoid).then_inc(score_ready, 1)
            act.wait_ge(gatesT_in_psum, 1)
            for b in range(B):
                act.activation(gatesT[:, b * S:(b + 1) * S], banks[b][0:E + 1, :], ACT.Copy).then_inc(gatesT_ready, 1)

            def shared():
                for n in range(B * NCH):
                    act.wait_ge(s_up_done, n + 1)
                    if n >= 2:
                        act.wait_ge(s_hid_ready, n - 1)
                    act.activation(shared_g[:, n % 2, :], banks[S_UP_BANKS[n % 2]][:], ACT.Gelu,
                                   bias=up_bias[:, E, n % NCH:n % NCH + 1], scale=1.0 / WSCALE).then_inc(s_gelu_done, 1)

            def x_high(j, k):
                act.wait_ge(xT_in_psum, j + 1)
                act.activation(xT_hi[:, k, :], banks[XT_BANKS[k]][:, 0:ET], ACT.Copy).then_inc(xT_hi_ready, 1)

            def gelu(j, k, first=False):
                for m in range(HALVES):
                    act.wait_ge(up_done, j * HALVES + (m + 1))
                    if not first:
                        act.wait_ge(hid_ready, j * HALVES + (m + 1 - SLOTS * HALVES))
                    for q in range(NCH // HALVES):
                        cols = slice(q * ET, (q + 1) * ET)
                        bias = tile_bias[:, bass.ds(j, 1), m * (NCH // HALVES) + q]
                        last = act.activation(hid[:, k, m, cols], banks[UP_BANK + HALVES * k + m][:, cols], ACT.Gelu,
                                              bias=bias, scale=1.0 / WSCALE)
                    last.then_inc(gelu_done, 1)

            def y_copy(j, k, i, first=False):
                act.wait_ge(y_done, j + 1)
                if not first:
                    act.wait_ge(y_row_out[k], i * (16 * PARTS))
                for n in range(PARTS):
                    last = act.activation(y_row[:, k, n], banks[Y_BANKS[k]][:, n * H:(n + 1) * H], ACT.Copy,
                                          scale=result_weight[:, bass.ds(j * PARTS + n, 1)])
                last.then_inc(y_row_ready, 1)

            shared()
            for k in range(SLOTS):
                x_high(k, k)
            act.wait_ge(tile_bias_ready, NCH)
            for k in range(SLOTS):
                gelu(k, k, first=True)
                x_high(k + SLOTS, k)
            for k in range(SLOTS):
                y_copy(k, k, 0, first=True)
                gelu(SLOTS + k, k)
                x_high(2 * SLOTS + k, k)
            with act.Fori(2, ROUNDS - 1) as i:
                for k in range(SLOTS):
                    j = i * SLOTS + k
                    y_copy(j - SLOTS, k, i - 1)
                    gelu(j, k)
                    x_high(j + SLOTS, k)
            for j in range(LOADED_TILES - SLOTS, EXPERT_TILES + SLOTS):
                if j == EXPERT_TILES:
                    act.wait_ge(place_kept, EXPERT_TILES)
                y_copy(j - SLOTS, j % SLOTS, (j - SLOTS) // SLOTS)
                if j < EXPERT_TILES:
                    gelu(j, j % SLOTS)

            for b in range(B):
                if POOL_TILES[b]:
                    act.wait_ge(tail, 2 * b + 2)
                    if b >= 2:
                        act.wait_ge(out_done[b % 2], 16 * (b // 2))
                for n in range(TPB - POOL_TILES[b], TPB):
                    act.activation(result[:, b % 2, n, :], total[:, b % 2, n, :], ACT.Copy,
                                   scale=inv_peak[:, b, n:n + 1]).then_inc(scaled_by_act, 1)

        @block.tensor
        def _(pe):
            pe.wait_ge(const_ready, 1)
            pe.wait_ge(ctx_ld, 16)
            for b in range(B):
                mm = pe.transpose(banks[7][:, b * SMALL:(b + 1) * SMALL], ctx_sb[:, b, :], ident[0:SMALL, 0:SMALL])
            mm.then_inc(ctxT_in_psum, 1)
            for b in range(B + 1):
                if b < B:
                    for n in range(TPB):
                        pe.wait_ge(y_ready, b * TPB + n + 1)
                        mm = pe.transpose(banks[b][:, n * P:(n + 1) * P], y[:, b * TPB + n, :], ident[:])
                    mm.then_inc(yT_in_psum, 1)
                if b:
                    if b == 1:
                        pe.wait_ge(ctxT_ready, 1)
                    pe.wait_ge(yT_ready, 2 * b - 1)
                    pe.matmul(banks[3 + b][0:SMALL, :], ctxm2T[:, b - 1, :], yT[:, b - 1, :], start=True, stop=False)
                    pe.wait_ge(yT_ready, 2 * b)
                    pe.matmul(banks[3 + b][0:SMALL, :], ones[:], ysqT[:, b - 1, :], start=False, stop=True
                              ).then_inc(d2_in_psum, 1)
            pe.wait_ge(small_ld, 16 * 6)
            pe.transpose(banks[0][:, 0:(E + 1) * NCH], bias_ld[:], ident[0:(E + 1) * NCH, 0:(E + 1) * NCH]
                         ).then_inc(biasT_in_psum, 1)
            for g in range(TPB):
                n = TPB - 1 - g
                pe.wait_ge(rows_in[g], 16)
                for b in range(B):
                    mm = pe.matmul(banks[g][:, b * P:(b + 1) * P], path_rows[:, b, n * P:(n + 1) * P],
                                   ctx_sb[:, b, :], start=True, stop=True)
                mm.then_inc(added_in_psum, 1)
            for g in range(TPB):
                pe.wait_ge(y2_ready, g + 1)
                for b, t in enumerate(group_list(g)):
                    if b == TPB - DVE_TILES[g]:
                        pe.wait_ge(y2_by_dve, sum(DVE_TILES[:g + 1]))
                    mm = pe.transpose(banks[4 + g][:, b * P:(b + 1) * P], y[:, t, :], ident[:])
                mm.then_inc(y2T_in_psum, 1)
            pe.wait_ge(weights_ready, 1)
            pe.wait_ge(x2_ready, B)
            for g in range(TPB):
                pe.wait_ge(y2T_lo_ready, g + 1)
                for t in group_list(g):
                    cols = slice(t * P, (t + 1) * P)
                    o = banks[0][:, t * E:(t + 1) * E]
                    pe.matmul(o, yT_hi[:, cols], gate_hi[:], start=True, stop=False)
                    pe.matmul(o, yT_hi[:, cols], gate_lo[:], start=False, stop=False)
                    mm = pe.matmul(o, yT_lo[:, cols], gate_hi[:], start=False, stop=True)
            mm.then_inc(logits_in_psum, 1)
            pe.wait_ge(picked_ready, 1)
            chosen = picked[:].rearrange("p n e -> p e n")
            pe.matmul(banks[4][:, 0:P], not_earlier[:], chosen, start=True, stop=True)
            pe.matmul(banks[5][:, 0:P], ones16[:], chosen, start=True, stop=True).then_inc(ranks_in_psum, 1)
            pe.wait_ge(gates_ready, 1)
            for t in range(TILES):
                mm = pe.transpose(banks[t // TPB][0:E + 1, t % TPB * P:(t % TPB + 1) * P], gates[:, t, :], ident[:])
            mm.then_inc(gatesT_in_psum, 1)
            pe.wait_ge(halves_lo, 2 * (E + 1))
            pe.wait_ge(slots_ready, 1)

            def three_passes(o, a_hi, a_lo, b_hi, b_lo, start, stop):
                pe.matmul(o, a_hi, b_hi, start=start, stop=False)
                pe.matmul(o, a_hi, b_lo, start=False, stop=False)
                return pe.matmul(o, a_lo, b_hi, start=False, stop=stop)

            def shared_up(b, c):
                n = b * NCH + c
                if n == 1:
                    pe.wait_ge(gatesT_ready, B)
                if n >= 2:
                    pe.wait_ge(s_gelu_done, n - 1)
                w = slice(E * I + c * P, E * I + (c + 1) * P)
                t = slice(b * S, (b + 1) * S)
                three_passes(banks[S_UP_BANKS[n % 2]][:], up_hi[:, w], up_lo[:, w], yT_hi[:, t], yT_lo[:, t],
                             True, True).then_inc(s_up_done, 1)

            def shared_down(b, n):
                if n == 0:
                    pe.wait_ge(s_hid_ready, (b + 1) * NCH)
                    if b > 1:
                        pe.wait_ge(acc_ready, b - 1)
                o = banks[S_DOWN_BANKS[b % 2]][:, n * H:(n + 1) * H]
                t = b * TPB + n
                pe.matmul(o, gatesT[:, t * P:(t + 1) * P], down_b_all[:], start=True, stop=False)
                for c in range(NCH):
                    w = slice(E * I + c * P, E * I + (c + 1) * P)
                    h = slice(n * P, (n + 1) * P)
                    mm = three_passes(o, shared_hi[:, b % S_SLOTS, c, h], shared_lo[:, b % S_SLOTS, c, h],
                                      down_hi[:, w], down_lo[:, w], False, c == NCH - 1)
                if n == TPB - 1:
                    mm.then_inc(s_down_done, 1)

            def shared():
                for m in range(B * NCH + S_LAG):
                    if m < B * NCH:
                        shared_up(m // NCH, m % NCH)
                    if m >= S_LAG:
                        shared_down((m - S_LAG) // TPB, (m - S_LAG) % TPB)

            expert_reg = [pe.alloc_register(f"expert{k}") for k in range(SLOTS)]

            def turn(j, k, r):
                pe.wait_ge(x_row_in[k], (r + 1) * 16)
                for n in range(PARTS):
                    mm = pe.transpose(banks[XT_BANKS[k]][:, n * P:(n + 1) * P], x_row[:, k, n, 0:H], ident[:])
                mm.then_inc(xT_in_psum, 1)

            def up(j, k):
                pe.reg_load(expert_reg[k], tile_expert[0:1, bass.ds(j, 1)])
                e = pe.snap(expert_reg[k], min_val=0, max_val=E - 1)
                pe.wait_ge(xT_ready, j + 1)
                for m in range(HALVES):
                    for q in range(NCH // HALVES):
                        c = m * (NCH // HALVES) + q
                        o = banks[UP_BANK + HALVES * k + m][:, q * ET:(q + 1) * ET]
                        w = bass.ds(e * I + c * P, P)
                        mm = three_passes(o, up_hi[:, w], up_lo[:, w], xT_hi[:, k, :], xT_lo[:, k, :], True, True)
                    mm.then_inc(up_done, 1)

            def down(j, k):
                e = pe.snap(expert_reg[k], min_val=0, max_val=E - 1)
                pe.wait_ge(hid_ready, j * HALVES + HALVES)
                for n in range(PARTS):
                    for c in range(NCH):
                        w = bass.ds(e * I + c * P, P)
                        m, q = c // (NCH // HALVES), c % (NCH // HALVES)
                        h = slice(q * ET + n * P, q * ET + (n + 1) * P)
                        mm = three_passes(banks[Y_BANKS[k]][:, n * H:(n + 1) * H], hid_hi[:, k, m, h], hid_lo[:, k, m, h],
                                          down_hi[:, w], down_lo[:, w], c == 0, c == NCH - 1)
                mm.then_inc(y_done, 1)

            shared()
            pe.wait_ge(table_ready, 1)
            pe.wait_ge(acc_ready, B)
            for k in range(SLOTS):
                turn(k, k, 0)
            for k in range(SLOTS):
                up(k, k)
                turn(SLOTS + k, k, 1)
            with pe.Fori(0, (LOADED_TILES - 2 * SLOTS) // UNROLL) as i:
                for u in range(UNROLL):
                    j, k = i * UNROLL + (SLOTS + u), u % SLOTS
                    down(j - SLOTS, k)
                    up(j, k)
                    turn(j + SLOTS, k, i * (UNROLL // SLOTS) + (2 + u // SLOTS))
            for j in range(LOADED_TILES - SLOTS, EXPERT_TILES + SLOTS):
                down(j - SLOTS, j % SLOTS)
                if j < EXPERT_TILES:
                    up(j, j % SLOTS)

        @block.vector
        def _(dve):
            def norm_stats(src, tiles, done, stats_sem, var_sem):
                for n in tiles:
                    ins = dve.bn_stats(stats[:, n, :], src[:, n, :])
                ins.then_inc(stats_sem, 1)
                dve.wait_ge(stats_sem, done + 1)
                for n in tiles:
                    ins = dve.bn_aggr(mv[:, n, :], stats[:, n, :])
                ins.then_inc(var_sem, 1)

            def norm_apply(src, b, sd_sem, rstd_sem, y_sem):
                t = batch_tiles(b)
                dve.wait_ge(sd_sem, b + 1)
                dve.reciprocal(rstd[:, t], sd[:, t]).then_inc(rstd_sem, 1)
                dve.wait_ge(rstd_sem, b + 1)
                for n in range(b * TPB, (b + 1) * TPB):
                    ins = dve.tensor_scalar(y[:, n, :], src[:, n, :], mv[:, n, 0:1], rstd[:, n:n + 1],
                                            ALU.subtract, ALU.mult)
                    if y_sem is y_ready:
                        ins.then_inc(y_sem, 1)
                if y_sem is not y_ready:
                    ins.then_inc(y_sem, 1)

            for b in range(B + 1):
                if b < B:
                    dve.wait_ge(x_in[b], 16)
                    norm_stats(x_sb, range(b * TPB, (b + 1) * TPB), b, stats_ready, var_ready)
                if b:
                    norm_apply(x_sb, b - 1, sd_ready, rstd_ready, y_ready)
            dve.wait_ge(aa_ready, B)
            for b in range(B):
                dve.wait_ge(d2_in_psum, b + 1)
                dve.tensor_scalar(dist[:, b, :], banks[4 + b][0:SMALL, :], aa[:, b:b + 1], 0.0, ALU.add, ALU.max
                                  ).then_inc(d2_ready, 1)

            dve.wait_ge(pads_ready, 1)
            dve.tensor_reduce(end_lane[:], ends[:], AX_X, ALU.max).then_inc(lanes_ready, 1)
            dve.wait_ge(lanes_ready, 1)
            dve.tensor_scalar(dsk[:, :, 0], best[:, :, 0], end_lane[:, 0:1], None, ALU.mult).then_inc(lanes_ready, 1)
            dve.tensor_scalar(cost[:, 0, 0:1], end_lane[:, 0:1], -BIG, BIG, ALU.mult, ALU.add
                              ).then_inc(lanes_ready, 1)
            dve.wait_ge(lanes_ready, 3)
            to_right = [min(lane + 1, 31) for lane in range(32)]
            to_left = [max(lane - 1, 0) for lane in range(32)]
            went_left, went_up, went_diag = mask_views(0, STEPS)
            dve.wait_ge(marks_ready, 1)
            for s in range(STEPS):
                if s:
                    dve.wait_ge(cost_ready, s)
                dve.stream_shuffle(edge[:, s % 2:s % 2 + 1], cost[:, s, W:W + 1], to_right).then_inc(inputs_ready, 1)
                dve.tensor_tensor(best[:, s, 1:W + 1], cost[:, s, 0:W], cost[:, s, 1:W + 1], ALU.min
                                  ).then_inc(inputs_ready, 1)
                if s:
                    dve.tensor_tensor(went_left[:, s - 1], cost[:, s, 0:W], best[:, s - 1, 1:W + 1], ALU.is_lt
                                      ).then_inc(compared, 1)
                if s in DIST_BOUNDS:
                    dve.wait_ge(dsk_in[DIST_BOUNDS.index(s)], 16)
                dve.wait_ge(inputs_ready, 2 * (s + 1))
                dve.tensor_tensor_scan(cost[:, s + 1, :], best[:, s, :], dsk[:, s, :], edge[:, s % 2:s % 2 + 1],
                                       ALU.min, ALU.add).then_inc(cost_ready, 1)
                dve.tensor_tensor(is_up[:, s], cost[:, s, 0:W], cost[:, s, 1:W + 1], ALU.is_gt)
            dve.wait_ge(cost_ready, STEPS)
            dve.tensor_tensor(went_left[:, STEPS - 1], cost[:, STEPS, 0:W], best[:, STEPS - 1, 1:W + 1], ALU.is_lt
                              ).then_inc(compared, 1)
            dve.tensor_scalar(goes_on[:, :, 0], best[:, :, 0], 0.0, end_lane[:, 1:2], ALU.mult, ALU.is_equal)
            dve.tensor_copy(inflow[:, 2:3], end_lane[:, 1:2]).then_inc(back_inputs_ready, 1)
            last = slice(MASK_BOUNDS[-1], STEPS)
            dve.wait_ge(compared, STEPS)
            dve.tensor_tensor(went_up[:, last], is_up[:, last], went_left[:, last], ALU.is_gt)
            dve.scalar_tensor_tensor(went_diag[:, last], went_left[:, last], -1.0, is_up[:, last], ALU.mult,
                                     ALU.is_equal).then_inc(last_mask, 1)
            dve.wait_ge(mask_ready, 3 * (len(MASK_BOUNDS) - 1))
            dve.wait_ge(last_mask, 1)
            for mask in (goes_on, leaves):
                dve.stream_shuffle(mask[:, 0:STEPS - 1, 1], mask[:, 1:STEPS, 2 * W + 1], to_left
                                   ).then_inc(marks_ready, 1)
            dve.wait_ge(marks_ready, 4)
            for n, s in enumerate(reversed(range(STEPS))):
                if n:
                    dve.wait_ge(path_ready, n)
                dve.stream_shuffle(edge[:, s % 2:s % 2 + 1], path[:, s + 1, 2 * W:2 * W + 1], to_left
                                   ).then_inc(back_inputs_ready, 1)
                if n:
                    dve.tensor_tensor(inflow[:].rearrange("l (k t) -> l k t", t=2),
                                      path[:, s + 1, 0::2].unsqueeze(2).to_broadcast([LANES, W + 1, 2]),
                                      leaves[:, s + 1, :].rearrange("l (k t) -> l k t", t=2), ALU.mult
                                      ).then_inc(back_inputs_ready, 1)
                dve.wait_ge(back_inputs_ready, 2 * (n + 1))
                dve.tensor_tensor_scan(path[:, s, 0:PAIRS - 1], goes_on[:, s, 0:PAIRS - 1], inflow[:, 0:PAIRS - 1],
                                       edge[:, s % 2:s % 2 + 1], ALU.mult, ALU.max).then_inc(path_ready, 1)

            for g in range(TPB + 1):
                if g < TPB:
                    t = group_tiles(g)
                    dve.wait_ge(added_in_psum, g + 1)
                    dve.tensor_tensor(x2[:, t, :], banks[g][:].rearrange("p (b d) -> p b d", d=H), x_sb[:, t, :], ALU.add
                                      ).then_inc(x2_ready, 1)
                    dve.wait_ge(x2_ready, g + 1)
                    norm_stats(x2, group_list(g), g, stats2_ready, var2_ready)
                if g:
                    t = group_tiles(g - 1)
                    dve.wait_ge(sd2_ready, g)
                    dve.reciprocal(rstd[:, t], sd[:, t]).then_inc(rstd2_ready, 1)
                    dve.wait_ge(rstd2_ready, g)
                    dve.scalar_tensor_tensor(shift[:, t], mv[:, t, 0], -1.0, rstd[:, t], ALU.mult, ALU.mult
                                             ).then_inc(shift_ready, 1)
                    for n in group_list(g - 1)[TPB - DVE_TILES[g - 1]:]:
                        dve.tensor_scalar(y[:, n, :], x2[:, n, :], mv[:, n, 0:1], rstd[:, n:n + 1], ALU.subtract,
                                          ALU.mult).then_inc(y2_by_dve, 1)
            for g in range(TPB):
                dve.wait_ge(y2T_hi_ready, g + 1)
                dve.tensor_tensor(tiles_of_yT(yT_lo, g), banks[4 + g][:].rearrange("p (b t) -> p b t", t=P),
                                  tiles_of_yT(yT_hi, g), ALU.subtract).then_inc(y2T_lo_ready, 1)

            def per_tile(v):
                return v.unsqueeze(2).to_broadcast([P, TILES, E])

            def per_expert(v):
                return v.unsqueeze(1).to_broadcast([P, TILES, E])

            def each_tile(v, n=TILES):
                return v.unsqueeze(2).to_broadcast([P, E, n])

            steps = [0]

            def routed(ins, meanwhile=None):
                steps[0] += 1
                ins.then_inc(route, 1)
                if meanwhile:
                    meanwhile()
                dve.wait_ge(route, steps[0])

            dve.wait_ge(logits_in_psum, 1)
            dve.scalar_tensor_tensor(logits[:], banks[0][:, 0:TILES * E].rearrange("p (n e) -> p n e", e=E),
                                     1.0 / WSCALE, per_expert(gate_b_sb[:]), ALU.mult, ALU.add).then_inc(logits_ready, 1)
            dve.wait_ge(score_ready, 1)
            for k, sc in enumerate((score, score2)):
                routed(dve.tensor_reduce(top[:, k, :], sc[:], AX_X, ALU.max))
                routed(dve.tensor_tensor(is_top[:], sc[:], per_tile(top[:, k, :]), ALU.is_equal))
                routed(dve.tensor_tensor_scan(met[:].rearrange("p n e -> p (n e)"), same_token[:].rearrange(
                    "p n e -> p (n e)"), is_top[:].rearrange("p n e -> p (n e)"), 0.0, ALU.mult, ALU.add))
                routed(dve.scalar_tensor_tensor(pick[:, k], met[:], 1.0, is_top[:], ALU.is_equal, ALU.mult))
                if k == 0:
                    routed(dve.scalar_tensor_tensor(score2[:], pick[:, 0], -4.0, score[:], ALU.mult, ALU.add))
            dve.tensor_tensor(picked[:], pick[:, 0], pick[:, 1], ALU.add).then_inc(picked_ready, 1)
            routed(dve.scalar_tensor_tensor(denom[:], top[:, 0, :], 1e-6, top[:, 1, :], ALU.add, ALU.add))
            routed(dve.reciprocal(denom[:], denom[:]))
            dve.wait_ge(ranks_in_psum, 1)
            routed(dve.tensor_tensor_scan(running[:].rearrange("p e n -> p (e n)"),
                                          carry_on[:].rearrange("p e n -> p (e n)"),
                                          banks[5][:, 0:P], 0.0, ALU.mult, ALU.add),
                   lambda: dve.tensor_tensor(weight[0], top[:, 0, :], denom[:], ALU.mult))
            routed(dve.tensor_tensor(exceeds[:], each_tile(running[:, :, TILES - 1], TILES_EACH),
                                     thresholds[:].unsqueeze(1).to_broadcast([P, E, TILES_EACH]), ALU.is_gt),
                   lambda: dve.tensor_tensor(weight[1], top[:, 1, :], denom[:], ALU.mult))
            routed(dve.tensor_reduce(tiles_of[:], exceeds[:], AX_X, ALU.add),
                   lambda: dve.tensor_tensor(offset[:], banks[4][:, 0:P].rearrange("p (e n) -> p e n", e=E), running[:],
                                             ALU.add).then_inc(aside_ready, 1))
            routed(dve.tensor_tensor_scan(tiles_upto[:], ones[:, 0:E], tiles_of[:], 0.0, ALU.mult, ALU.add))
            routed(dve.tensor_tensor(tiles_before[:], tiles_upto[:], tiles_of[:], ALU.subtract))
            dve.wait_ge(aside_ready, 1)
            routed(dve.scalar_tensor_tensor(place[:].rearrange("p n e -> p e n"), each_tile(tiles_before[:]), float(ET),
                                            offset[:], ALU.mult, ALU.add))
            routed(dve.tensor_tensor(part[:, 0], pick[:, 0], place[:], ALU.mult),
                   lambda: dve.tensor_tensor(part[:, 1], pick[:, 1], place[:], ALU.mult).then_inc(aside_ready, 1))
            with nc.allow_low_precision(reason="one whole number and zeros"):
                for k in range(TOP):
                    if k:
                        dve.wait_ge(aside_ready, 2)
                    dve.tensor_reduce(slot[:, k * TILES:(k + 1) * TILES], part[:, k], AX_X, ALU.add
                                      ).then_inc(slots_ready, 1)
            dve.wait_ge(slots_ready, 2)
            for k in range(TOP):
                routed(dve.scalar_tensor_tensor(part[:, k], pick[:, k], WSCALE, per_tile(weight[k]),
                                                ALU.mult, ALU.mult))
            dve.tensor_tensor(gates[:, :, 0:E], part[:, 0], part[:, 1], ALU.add).then_inc(gates_ready, 1)
            def every_tile(v):
                return v.unsqueeze(1).to_broadcast([P, EXPERT_TILES, E])

            tile_nos = tile_no[:].unsqueeze(2).to_broadcast([P, EXPERT_TILES, E])
            routed(dve.tensor_tensor(past[:], every_tile(tiles_upto[:]), tile_nos, ALU.is_le))
            routed(dve.tensor_reduce(tile_expert_f[:], past[0:1], AX_X, ALU.add))
            dve.tensor_scalar(tile_expert[:], tile_expert_f[:], float(E - 1), None, ALU.min).then_inc(table_ready, 1)
            def shared():
                def keep_sum(b):
                    dve.wait_ge(s_down_done, b + 1)
                    dve.tensor_copy(acc[:, b * S:(b + 1) * S], banks[S_DOWN_BANKS[b % 2]][:]).then_inc(acc_ready, 1)

                for n in range(B * NCH):
                    b, c = n // NCH, n % NCH
                    if c == 0 and b >= S_SLOTS:
                        keep_sum(b - S_SLOTS)
                    dve.wait_ge(s_gelu_done, n + 1)
                    dve.tensor_copy(shared_hi[:, b % S_SLOTS, c, :], shared_g[:, n % 2, :]).then_inc(s_hi_ready, 1)
                    dve.wait_ge(s_hi_ready, n + 1)
                    dve.tensor_tensor(shared_lo[:, b % S_SLOTS, c, :], shared_g[:, n % 2, :],
                                      shared_hi[:, b % S_SLOTS, c, :], ALU.subtract).then_inc(s_hid_ready, 1)

                keep_sum(B - S_SLOTS)
                routed(dve.tensor_tensor(started[:], every_tile(tiles_before[:]), tile_nos, ALU.is_le))
                routed(dve.tensor_tensor(started[:], started[:], past[:], ALU.subtract))
                dve.wait_ge(up_bias_ready, 1)
                for c in range(NCH):
                    routed(dve.tensor_tensor(past[:], started[:], every_tile(up_bias[:, 0:E, c]), ALU.mult))
                    ins = dve.tensor_reduce(tile_bias[:, :, c], past[:], AX_X, ALU.add)
                    ins.then_inc(tile_bias_ready, 1)
                    dve.wait_ge(tile_bias_ready, c + 1)
                for b in range(B - S_SLOTS + 1, B):
                    keep_sum(b)

            def x_low(j, k):
                dve.wait_ge(xT_hi_ready, j + 1)
                dve.tensor_tensor(xT_lo[:, k, :], banks[XT_BANKS[k]][:, 0:ET], xT_hi[:, k, :], ALU.subtract
                                  ).then_inc(xT_ready, 1)

            def hidden_halves(j, k, first=False):
                for m in range(HALVES):
                    dve.wait_ge(gelu_done, j * HALVES + (m + 1))
                    if m == 0 and not first:
                        dve.wait_ge(y_done, j - 1)
                    dve.tensor_copy(hid_hi[:, k, m, :], hid[:, k, m, :]).then_inc(hid_hi_ready, 1)
                    dve.wait_ge(hid_hi_ready, j * HALVES + (m + 1))
                    dve.tensor_tensor(hid_lo[:, k, m, :], hid[:, k, m, :], hid_hi[:, k, m, :], ALU.subtract
                                      ).then_inc(hid_ready, 1)

            shared()
            for k in range(SLOTS):
                x_low(k, k)
            for k in range(SLOTS):
                hidden_halves(k, k, first=True)
                x_low(SLOTS + k, k)
            with dve.Fori(1, ROUNDS - 1) as i:
                for k in range(SLOTS):
                    hidden_halves(i * SLOTS + k, k)
                    x_low(i * SLOTS + (k + SLOTS), k)
            for j in range(LOADED_TILES - SLOTS, EXPERT_TILES):
                hidden_halves(j, j % SLOTS)

            def add_shared(b):
                dve.wait_ge(pair_ready, b + 1)
                if b >= 2:
                    dve.wait_ge(result_ready, b - 1)
                    if sum(POOL_TILES[:b - 1]):
                        dve.wait_ge(result_by_pool, sum(POOL_TILES[:b - 1]))
                dve.tensor_tensor(total[:, b % 2].rearrange("p n d -> p (n d)"), by_token[0][:, b * S:(b + 1) * S],
                                  acc[:, b * S:(b + 1) * S], ALU.add).then_inc(total_ready, 1)

            def find_peak(b):
                dve.wait_ge(total_ready, b + 1)
                dve.tensor_reduce(peak[:, b, :], total[:, b % 2], AX_X, ALU.max, apply_absolute_value=True
                                  ).then_inc(peak_ready, 1)

            add_shared(0)
            find_peak(0)
            for b in range(B):
                dve.wait_ge(peak_ready, b + 1)
                dve.tensor_scalar(peak_eps[:, b, :], peak[:, b, :], 1e-6 * WSCALE / OUT_SCALE, None, ALU.add
                                  ).then_inc(tail, 1)
                if b + 1 < B:
                    add_shared(b + 1)
                dve.wait_ge(tail, 2 * b + 1)
                dve.reciprocal(inv_peak[:, b, :], peak_eps[:, b, :]).then_inc(tail, 1)
                if b + 1 < B:
                    find_peak(b + 1)
                dve.wait_ge(tail, 2 * b + 2)
                if b >= 2:
                    dve.wait_ge(out_done[b % 2], 16 * (b // 2))
                for n in range(TPB - POOL_TILES[b]):
                    ins = dve.scalar_tensor_tensor(result[:, b % 2, n, :], total[:, b % 2, n, :],
                                                   inv_peak[:, b, n:n + 1], x2[:, b * TPB + n, :], ALU.mult, ALU.add)
                ins.then_inc(result_ready, 1)


_INS = ["x", "ctx_1024"] + ["L0_ffn_" + n for n in ("gate_w", "bias", "up_w", "up_b", "down_w", "down_b",
                                                   "sw_up", "sb_up", "sw_down", "sb_down")]


def kernel(**inputs):
    import numpy as np
    import concourse.bacc as bacc
    from concourse.bass_utils import run_bass_kernel_spmd

    nc = bacc.Bacc("TRN2", target_bir_lowering=False, num_devices=1)
    arrays, args = {}, []
    for name in _INS:
        a = np.ascontiguousarray(inputs[name])
        arrays[f"in_{name}"] = a
        args.append(nc.dram_tensor(f"in_{name}", a.shape, mybir.dt.from_np(a.dtype), kind="ExternalInput").ap())
    args.append(nc.dram_tensor("out_0", (B, S, H), F32, kind="ExternalOutput").ap())
    build(nc, *args)
    r = run_bass_kernel_spmd(nc, [arrays], core_ids=[0])
    return r.results[0]["out_0"]
```
